# Optimizing a Trainium2 kernel written in Bass

```python
import numpy as np
import jax
import jax.numpy as jnp

def _softmax(x, axis=-1):
    return jax.nn.softmax(x, axis=axis)

def _gelu(x):
    return jax.nn.gelu(x, approximate=True)

def _silu(x):
    return jax.nn.silu(x)

def _sigmoid(x):
    return jax.nn.sigmoid(x)

def _layernorm(x, axis=-1, eps=1e-05):
    m = jnp.mean(x, axis=axis, keepdims=True)
    v = jnp.var(x, axis=axis, keepdims=True)
    return (x - m) / jnp.sqrt(v + eps)

def _scatter_add(tgt, idx, src, axis=0):
    return tgt.at[idx].add(src)

def _segment_sum(src, seg, n):
    return jax.ops.segment_sum(src, seg, n)
kernel_name = 'mk_gnn_preln_d4_gnn_r8_049a5c'

def setup_inputs(seed: int=0):
    np.random.seed(seed)
    _w = jnp.asarray

    def _rec_inputs():
        import jax
        import jax.numpy as jnp
        _gk = jax.random.key(seed)
        x = -0.000202 + 1 * jax.random.normal(jax.random.fold_in(_gk, 1), (12500, 64), jnp.float32)
        _s = jax.random.randint(jax.random.fold_in(_gk, 2), (200000,), 0, 12500, jnp.int32)
        _d = jax.random.randint(jax.random.fold_in(_gk, 3), (200000,), 0, 12500, jnp.int32)
        _loop = jnp.arange(12500, dtype=jnp.int32)
        src = jnp.concatenate([_s, _d, _loop])
        dst = jnp.concatenate([_d, _s, _loop])
        _o = jnp.argsort(dst, stable=True)
        src = src[_o]
        dst = dst[_o]
        edge_attr_32 = -5.16925e-05 + 1.00005 * jax.random.normal(jax.random.fold_in(_gk, 13), (412500, 32), jnp.float32)
        edge_type_8 = jax.random.randint(jax.random.fold_in(_gk, 15), (412500,), 0, 8, jnp.int32)
        edge_weight1 = 0.000109407 + 1.00012 * jax.random.normal(jax.random.fold_in(_gk, 16), (412500, 1), jnp.float32)
        return (x, src, dst, edge_attr_32, edge_type_8, edge_weight1)
    x, src, dst, edge_attr_32, edge_type_8, edge_weight1 = _rec_inputs()

    def _L0_gnn_setup():
        import jax, jax.numpy as jnp
        import numpy as np
        N_NODES = 12500
        N_EDGES = 156250
        D_IN = 64
        D_OUT = 64
        key = jax.random.key(seed)
        k_h, k_e, k_src, k_dst, k_w, k_b = jax.random.split(key, 6)
        h = jax.random.normal(k_h, (N_NODES, D_IN), dtype=jnp.float32)
        e = jax.random.normal(k_e, (N_EDGES, 1), dtype=jnp.float32)
        src = jax.random.randint(k_src, (N_EDGES,), 0, N_NODES, dtype=jnp.int64)
        dst = jax.random.randint(k_dst, (N_EDGES,), 0, N_NODES, dtype=jnp.int64)
        W = jax.random.normal(k_w, (D_OUT, D_IN), dtype=jnp.float32) / np.sqrt(D_IN)
        b = jax.random.normal(k_b, (D_OUT,), dtype=jnp.float32) * 0.01
        return {'h': h, 'e': e, 'src': src, 'dst': dst, 'W': W, 'b': b}
    _L0_gnn_all = _L0_gnn_setup()
    _L0_gnn_in = {k: v for k, v in _L0_gnn_all.items() if k in ('W', 'b')}
    del _L0_gnn_all

    def _L1_gnn_setup():
        import jax, jax.numpy as jnp
        import numpy as np
        N_NODES = 12500
        N_EDGES = 400000
        EDGE_OUT = 32
        HID = 128
        NODE_OUT = 64
        N_GRAPHS = 16
        key = jax.random.key(seed)
        ks = jax.random.split(key, 9)
        x = jax.random.normal(ks[0], (N_NODES, 64), dtype=jnp.float32)
        edge_index = jax.random.randint(ks[1], (2, N_EDGES), 0, N_NODES, dtype=jnp.int64)
        edge_attr = jax.random.normal(ks[2], (N_EDGES, EDGE_OUT), dtype=jnp.float32)
        u = jax.random.normal(ks[3], (N_GRAPHS, 1), dtype=jnp.float32)
        batch = jnp.sort(jax.random.randint(ks[4], (N_NODES,), 0, N_GRAPHS, dtype=jnp.int64))
        d_in = 3 * EDGE_OUT + 1
        W1 = jax.random.normal(ks[5], (d_in, HID), dtype=jnp.float32) / np.sqrt(d_in)
        b1 = jnp.zeros((HID,), dtype=jnp.float32)
        W2 = jax.random.normal(ks[6], (HID, NODE_OUT), dtype=jnp.float32) / np.sqrt(HID)
        b2 = jnp.zeros((NODE_OUT,), dtype=jnp.float32)
        return {'x': x, 'edge_index': edge_index, 'edge_attr': edge_attr, 'u': u, 'batch': batch, 'W1': W1, 'b1': b1, 'W2': W2, 'b2': b2}
    _L1_gnn_all = _L1_gnn_setup()
    _L1_gnn_in = {k: v for k, v in _L1_gnn_all.items() if k in ('u', 'W1', 'b1', 'W2', 'b2')}
    del _L1_gnn_all

    def _L2_gnn_setup():
        import jax, jax.numpy as jnp
        import numpy as np
        N_NODES = 6250
        N_EDGES = 100000
        FEAT_DIM = 64
        NUM_RELS = 8
        key = jax.random.key(seed)
        k1, k2, k3, k4, k5 = jax.random.split(key, 5)
        features = jax.random.normal(k1, (N_NODES, FEAT_DIM), dtype=jnp.float32)
        limit = np.sqrt(2.0) * np.sqrt(6.0 / (FEAT_DIM + FEAT_DIM))
        weight_r = jax.random.uniform(k2, (NUM_RELS, FEAT_DIM, FEAT_DIM), dtype=jnp.float32, minval=-limit, maxval=limit)
        src = jax.random.randint(k3, (N_EDGES,), 0, N_NODES, dtype=jnp.int64 if jax.config.jax_enable_x64 else jnp.int32)
        dst = jax.random.randint(k4, (N_EDGES,), 0, N_NODES, dtype=src.dtype)
        etype = jax.random.randint(k5, (N_EDGES,), 0, NUM_RELS, dtype=src.dtype)
        return {'features': features, 'weight_r': weight_r, 'src': src, 'dst': dst, 'etype': etype}
    _L2_gnn_all = _L2_gnn_setup()
    _L2_gnn_in = {k: v for k, v in _L2_gnn_all.items() if k in ('weight_r',)}
    del _L2_gnn_all

    def _L3_gnn_setup():
        import jax, jax.numpy as jnp
        import numpy as np
        N_NODES = 6250
        N_EDGES = 200000
        D_FEAT = 64
        NEG_SLOPE = 0.2
        key = jax.random.key(seed)
        k1, k2, k3, k4, k5 = jax.random.split(key, 5)
        z = jax.random.normal(k1, (N_NODES, D_FEAT), dtype=jnp.float32)
        attn_l = jax.random.normal(k2, (D_FEAT,), dtype=jnp.float32) * 0.1
        attn_r = jax.random.normal(k3, (D_FEAT,), dtype=jnp.float32) * 0.1
        src = jax.random.randint(k4, (N_EDGES,), 0, N_NODES, dtype=jnp.int32)
        dst = jax.random.randint(k5, (N_EDGES,), 0, N_NODES, dtype=jnp.int32)
        return {'z': z, 'attn_l': attn_l, 'attn_r': attn_r, 'src': src, 'dst': dst}
    _L3_gnn_all = _L3_gnn_setup()
    _L3_gnn_in = {k: v for k, v in _L3_gnn_all.items() if k in ('attn_l', 'attn_r')}
    del _L3_gnn_all
    return {'x': x, 'src': src, 'dst': dst, 'edge_attr_32': edge_attr_32, 'edge_type_8': edge_type_8, 'edge_weight1': edge_weight1, 'L0_gnn_W': _L0_gnn_in['W'], 'L0_gnn_b': _L0_gnn_in['b'], 'L1_gnn_u': _L1_gnn_in['u'], 'L1_gnn_W1': _L1_gnn_in['W1'], 'L1_gnn_b1': _L1_gnn_in['b1'], 'L1_gnn_W2': _L1_gnn_in['W2'], 'L1_gnn_b2': _L1_gnn_in['b2'], 'L2_gnn_weight_r': _L2_gnn_in['weight_r'], 'L3_gnn_attn_l': _L3_gnn_in['attn_l'], 'L3_gnn_attn_r': _L3_gnn_in['attn_r']}

def reference(x, src, dst, edge_attr_32, edge_type_8, edge_weight1, L0_gnn_W, L0_gnn_b, L1_gnn_u, L1_gnn_W1, L1_gnn_b1, L1_gnn_W2, L1_gnn_b2, L2_gnn_weight_r, L3_gnn_attn_l, L3_gnn_attn_r):
    import jax
    import jax.numpy as jnp

    def _L0_gnn_ref(h, e, src, dst, W, b):
        import jax, jax.numpy as jnp
        import numpy as np
        N_NODES = 12500
        N_EDGES = 156250
        D_IN = 64
        D_OUT = 64
        m = h[src] * e
        ft = jax.ops.segment_sum(m, dst, num_segments=N_NODES)
        return ft @ W.T + b

    def _L1_gnn_ref(x, edge_index, edge_attr, u, batch, W1, b1, W2, b2):
        import jax, jax.numpy as jnp
        import numpy as np
        N_NODES = 12500
        N_EDGES = 400000
        EDGE_OUT = 32
        HID = 128
        NODE_OUT = 64
        N_GRAPHS = 16
        N = x.shape[0]
        row = edge_index[0]
        seg_sum = jax.ops.segment_sum(edge_attr, row, num_segments=N)
        seg_max = jax.ops.segment_max(edge_attr, row, num_segments=N)
        cnt = jax.ops.segment_sum(jnp.ones((edge_attr.shape[0], 1), edge_attr.dtype), row, num_segments=N)
        seg_mean = seg_sum / jnp.maximum(cnt, 1.0)
        seg_max = jnp.where(cnt > 0, seg_max, 0.0)
        h = jnp.concatenate([seg_sum, seg_max, seg_mean, u[batch]], axis=1)
        h = jax.nn.relu(h @ W1 + b1)
        return h @ W2 + b2

    def _L2_gnn_ref(features, weight_r, src, dst, etype):
        import jax, jax.numpy as jnp
        import numpy as np
        N_NODES = 6250
        N_EDGES = 100000
        FEAT_DIM = 64
        NUM_RELS = 8
        N, D = features.shape
        c = 0.2
        deg = jax.ops.segment_sum(jnp.ones(dst.shape, dtype=features.dtype), dst, num_segments=N)
        hw = jnp.einsum('nd,rdf->rnf', features, weight_r)
        msg = hw[etype, src] / deg[dst][:, None]
        M = jax.ops.segment_sum(msg, dst, num_segments=N)
        updated = jax.nn.relu(c * features + (1.0 - c) * M)
        return jnp.where((deg > 0)[:, None], updated, features)

    def _L3_gnn_ref(z, attn_l, attn_r, src, dst):
        import jax, jax.numpy as jnp
        import numpy as np
        N_NODES = 6250
        N_EDGES = 200000
        D_FEAT = 64
        NEG_SLOPE = 0.2
        n = z.shape[0]
        el = z @ attn_l
        er = z @ attn_r
        e = jax.nn.leaky_relu(el[src] + er[dst], negative_slope=NEG_SLOPE)
        m = jax.ops.segment_max(e, dst, num_segments=n)
        ex = jnp.exp(e - m[dst])
        den = jax.ops.segment_sum(ex, dst, num_segments=n)
        a = ex / den[dst]
        msg = z[src] * a[:, None]
        rst = jax.ops.segment_sum(msg, dst, num_segments=n)
        return jax.nn.elu(rst)
    edge_index = jnp.stack([src, dst])
    batch0 = jnp.zeros((12500,), jnp.int32)
    h = jnp.maximum(_layernorm(x, axis=-1), 0.0)
    x = x + _L0_gnn_ref(h, edge_weight1, src, dst, L0_gnn_W, L0_gnn_b)
    h = jnp.maximum(_layernorm(x, axis=-1), 0.0)
    x = x + _L1_gnn_ref(h, edge_index, edge_attr_32, L1_gnn_u, batch0, L1_gnn_W1, L1_gnn_b1, L1_gnn_W2, L1_gnn_b2)
    h = jnp.maximum(_layernorm(x, axis=-1), 0.0)
    x = x + _L2_gnn_ref(h, L2_gnn_weight_r, src, dst, edge_type_8)
    h = jnp.maximum(_layernorm(x, axis=-1), 0.0)
    x = x + _L3_gnn_ref(h, L3_gnn_attn_l, L3_gnn_attn_r, src, dst)
    return x

_drawn_inputs = setup_inputs


def setup_inputs(seed=0):
    import zlib

    import numpy as np

    out = dict(_drawn_inputs(seed))
    spreads = {'L1_gnn_b1': (0.0, 0.528), 'L1_gnn_b2': (0.0, 0.305)}
    factors = {'L0_gnn_b': 21.99, 'L1_gnn_u': 5.281, 'L3_gnn_attn_l': 8.0, 'L3_gnn_attn_r': 8.0}
    for name, (base, spread) in spreads.items():
        noise = np.random.default_rng([zlib.crc32(name.encode()), seed]).standard_normal(out[name].shape)
        drawn = base * np.exp(spread * noise) if base else spread * noise
        out[name] = jnp.asarray(drawn.astype(out[name].dtype))
    for name, factor in factors.items():
        out[name] = (out[name] * factor).astype(out[name].dtype)
    return out
```

```python
import concourse.bass as bass
from concourse import mybir
from contextlib import ExitStack

P = 128
D = 64
A = 32
HID = 128
LOW = -1.7e38
F32 = mybir.dt.float32
BF16 = mybir.dt.bfloat16
I32 = mybir.dt.int32
ALU = mybir.AluOpType
ACT = mybir.ActivationFunctionType
AX = mybir.AxisListType.X


class Steps:

    def __init__(self, engine, sem):
        self.engine, self.sem, self.count = engine, sem, 0

    def done(self, instruction):
        self.count += 1
        instruction.then_inc(self.sem, 1)
        self.engine.wait_ge(self.sem, self.count)


def build(nc, x, src, dst, etype, weight, attr, W0, b0, u, W1, b1, W2, b2, Wr, attn_l, attn_r, out, L):
    J = src.shape[1]
    NCH = J // L
    EP = P * J
    N = out.shape[0]
    HT = x.shape[0] // P
    NP = HT * P
    R = Wr.shape[0]
    TG = 7
    NG = HT // TG
    HL = L // 2
    FM = D + 2
    assert NCH % 2 == 0 and HT % TG == 0 and L % 2 == 0 and NP > N

    h_table = nc.dram_tensor("h_table", [NP, D], F32, kind="Internal").ap()
    rel_table = nc.dram_tensor("rel_table", [R * NP, D], F32, kind="Internal").ap()
    att_table = nc.dram_tensor("att_table", [NP, D + 1], F32, kind="Internal").ap()
    er_table = nc.dram_tensor("er_table", [NP, 1], F32, kind="Internal").ap()
    er_start = nc.dram_tensor("er_start", [EP + NP, 1], F32, kind="Internal").ap()
    scan_wsum = nc.dram_tensor("scan_wsum", [EP + 1, D], F32, kind="Internal").ap()
    scan_pool = nc.dram_tensor("scan_pool", [EP + 1, D], F32, kind="Internal").ap()
    scan_rel = nc.dram_tensor("scan_rel", [EP + 1, D], F32, kind="Internal").ap()
    scan_att = nc.dram_tensor("scan_att", [EP + 1, FM], F32, kind="Internal").ap()
    by_src = nc.dram_tensor("by_src", [EP + 2, A + 1], F32, kind="Internal").ap()

    ctx = ExitStack()
    with ctx:
        def sb(name, shape, dt=F32, c=ctx):
            return c.enter_context(nc.sbuf_tensor(name, shape, dt))

        def ps(name, shape, dt=F32, c=ctx):
            return c.enter_context(nc.psum_tensor(name, shape, dt))

        phase_sems = []

        def semaphore(name, c=None):
            if c is None:
                return ctx.enter_context(nc.semaphore(name))
            phase_sems.append(c.enter_context(nc.semaphore(name)))
            return phase_sems[-1]

        def clear_semaphores():
            used = list(phase_sems)
            phase_sems.clear()
            with nc.Block() as block:
                @block.sync
                def _(sp):
                    for s in used:
                        sp.sem_clear(s)

        def phase(c):
            c.callback(clear_semaphores)
            return c.enter_context(nc.Block())

        X = sb("X", [P, HT, D])
        H = sb("H", [P, HT, D])
        ident = sb("ident", [P, P])
        count_src = sb("count_src", [P, HT])
        count_dst = sb("count_dst", [P, HT])
        first_src = sb("first_src", [P, HT])
        first_dst = sb("first_dst", [P, HT])
        end_src = sb("end_src", [P, HT], I32)
        end_dst = sb("end_dst", [P, HT], I32)
        iota_b = sb("iota_b", [P, P], BF16)
        below_b = sb("below_b", [P, P], F32)
        stat = sb("stat", [P, 4, HT])
        small = sb("small", [P, 16])
        zero_row = sb("zero_row", [1, FM])

        def vector_norm(dve, steps, scratch, var_ready, root_ready):
            mean, var, root = (stat[:, k, :] for k in range(3))
            wide = lambda a: a.unsqueeze(2).to_broadcast([P, HT, D])
            steps.done(nc.vector.tensor_reduce(mean, X[:], AX, ALU.add))
            steps.done(nc.vector.tensor_scalar(mean, mean, 1.0 / D, None, ALU.mult))
            steps.done(nc.vector.tensor_tensor(H[:], X[:], wide(mean), ALU.subtract))
            steps.done(nc.vector.tensor_tensor(scratch, H[:], H[:], ALU.mult))
            steps.done(nc.vector.tensor_reduce(var, scratch, AX, ALU.add))
            nc.vector.tensor_scalar(var, var, 1.0 / D, 1e-5, ALU.mult, ALU.add).then_inc(var_ready, 1)
            dve.wait_ge(root_ready, 1)
            steps.done(nc.vector.reciprocal(root, root))
            return nc.vector.scalar_tensor_tensor(H[:], H[:], 0.0, wide(root), ALU.max, ALU.mult)

        def scalar_norm(act, var_ready, root_ready):
            act.wait_ge(var_ready, 1)
            nc.scalar.activation(stat[:, 2, :], stat[:, 1, :], ACT.Sqrt).then_inc(root_ready, 1)

        with ExitStack() as c:
            scratch = sb("scratch", [P, HT, D], c=c)
            iota_i = sb("iota_i", [P, P], c=c)
            zeros = sb("zeros", [P, J], c=c)
            sentinel = sb("sentinel", [1, 2 * (A + 1)], c=c)
            s_x, s_made, s_filled, s_steps, s_var, s_root, s_h, s_table = (
                semaphore(n, c) for n in
                ("x_loaded", "consts_made", "filled", "norm_steps", "var_ready", "root_ready", "h_ready", "table_stored"))
            block = phase(c)

            @block.gpsimd
            def _(pool):
                nc.gpsimd.iota(iota_i[:], [[1, P]], base=0, channel_multiplier=0,
                               allow_small_or_imprecise_dtypes=True).then_inc(s_made, 1)
                nc.gpsimd.memset(ident[:], 1.0).then_inc(s_made, 1)
                nc.gpsimd.memset(below_b[:], 1.0).then_inc(s_made, 1)
                pool.wait_ge(s_made, 3)
                nc.gpsimd.affine_select(out=ident[:], in_=ident[:], compare_op=ALU.is_equal, fill=0.0, base=0,
                                        pattern=[[1, P]], channel_multiplier=-1).then_inc(s_made, 1)
                nc.gpsimd.affine_select(out=below_b[:], in_=below_b[:], compare_op=ALU.is_gt, fill=0.0, base=0,
                                        pattern=[[1, P]], channel_multiplier=-1).then_inc(s_made, 1)

            @block.vector
            def _(dve):
                nc.vector.memset(zero_row[:], 0.0).then_inc(s_filled, 1)
                nc.vector.memset(zeros[:], 0.0).then_inc(s_filled, 1)
                nc.vector.memset(sentinel[:, 0:A + 1], -1.0).then_inc(s_filled, 1)
                nc.vector.memset(sentinel[:, A + 1:], -2.0).then_inc(s_filled, 1)
                dve.wait_ge(s_made, 5)
                nc.vector.tensor_copy(iota_b[:], iota_i[:])
                dve.wait_ge(s_x, 16)
                steps = Steps(dve, s_steps)
                vector_norm(dve, steps, scratch[:], s_var, s_root).then_inc(s_h, 1)

            @block.scalar
            def _(act):
                scalar_norm(act, s_var, s_root)

            @block.sync
            def _(sp):
                sp.dma_start(X[:], x.rearrange("(h p) d -> p h d", p=P)).then_inc(s_x, 16)
                sp.wait_ge(s_filled, 4)
                n = 0
                for rows in (scan_wsum, scan_pool, scan_rel):
                    sp.dma_start(rows[EP:EP + 1, :], zero_row[0:1, 0:D]).then_inc(s_table, 16)
                    n += 16
                sp.dma_start(scan_att[EP:EP + 1, :], zero_row[0:1, :]).then_inc(s_table, 16)
                sp.dma_start(er_start[0:EP, :].rearrange("(p j) o -> p (j o)", p=P), zeros[:]).then_inc(s_table, 16)
                sp.dma_start(by_src[0:1, :], sentinel[0:1, 0:A + 1]).then_inc(s_table, 16)
                sp.dma_start(by_src[EP + 1:EP + 2, :], sentinel[0:1, A + 1:]).then_inc(s_table, 16)
                sp.wait_ge(s_h, 1)
                sp.dma_start(h_table.rearrange("(h p) d -> p h d", p=P), H[:]).then_inc(s_table, 16)
                sp.wait_ge(s_table, n + 16 * 5)

        def gathered_layer(kind, table, width, rows_out):
            F = FM if kind == "att" else D
            NAME = kind
            with ExitStack() as c:
                def slots(name, shape, dt=F32):
                    return [sb(f"{NAME}_{name}{s}", shape, dt, c) for s in range(2)]

                def sem(name):
                    return semaphore(f"{NAME}_{name}", c)

                G = slots("G", [P, L, width])
                S = slots("S", [P, L, F])
                idx = slots("idx", [P, L], I32)
                keys = slots("keys", [P, L + 1], I32)
                same = slots("same", [P, L])
                loaded = [sem(f"loaded{s}") for s in range(2)]
                gathered = [semaphore(f"{kind}_gathered{s}") for s in range(2)]
                stored = [sem(f"stored{s}") for s in range(2)]
                same_ready, scanned, issuing = sem("same_ready"), sem("scanned"), sem("issuing")
                PRIMED = 3 if kind == "att" else 2
                if kind == "wsum":
                    wt = slots("wt", [P, L])
                    weighed = sem("weighed")
                    parts_i = sb("parts_i", [P, 4, L], I32, c)
                    parts = sb("parts", [P, 4, L], F32, c)
                    OH = sb("OH", [P, 2, 2, HL, P], BF16, c)
                    zero_b = sb("zero_b", [P, P], BF16, c)
                    C = [ps("C_src", [P, 512], c=c), ps("C_dst", [P, 512], c=c)]
                    split, floated = sem("keys_split"), sem("keys_floated")
                    oh_ready, oh_used, zeroed, counted = (
                        sem("onehot_ready"), sem("onehot_used"), sem("zeroed"), sem("counted"))
                if kind == "rel":
                    ty = slots("ty", [P, L], I32)
                    idx_ready = sem("idx_ready")
                if kind == "att":
                    er_in = slots("er_in", [P, L])
                    er = slots("er", [P, L])
                    cut = slots("cut", [P, L])
                    score = slots("score", [P, L])
                    top = slots("top", [P, L + 1])
                    held = slots("held", [P, L])
                    ex = slots("ex", [P, 2, L])
                    er_first = sb("er_first", [P, 1], F32, c)
                    key_first = sb("key_first", [P, 1], I32, c)
                    er_fetched, key_loaded = semaphore("er_fetched"), sem("key_loaded")
                    att_step, ex_ready, exped = sem("att_step"), sem("ex_ready"), sem("exped")
                block = phase(c)
                key_cols = lambda off, at, n: dst[off:EP + off].rearrange("(p j) -> p j", p=P)[:, bass.ds(at, n)]

                @block.sync
                def _(sp):
                    if kind == "att":
                        sp.dma_start(key_first[:], dst[1:1 + EP].rearrange("(p j) -> p j", p=P)[:, 0:1], allow_slow_non_contiguous=True).then_inc(key_loaded, 16)
                    with sp.Fori(0, NCH // 2) as i:
                        for s in range(2):
                            at = (2 * i + s) * L
                            sp.wait_ge(scanned, 2 * i + s + PRIMED - 1)
                            sp.dma_start(keys[s][:, 0:L], key_cols(0, at, L)).then_inc(loaded[s], 16)
                            sp.dma_start(keys[s][:, L:L + 1], key_cols(1, at + L - 1, 1), allow_slow_non_contiguous=True).then_inc(loaded[s], 16)
                            if kind == "rel":
                                sp.dma_start(ty[s][:], etype[:, bass.ds(at, L)]).then_inc(loaded[s], 16)
                            if kind == "wsum":
                                sp.dma_start(wt[s][:], weight[:, bass.ds(at, L)]).then_inc(loaded[s], 16)
                            if kind == "att":
                                sp.dma_start(er_in[s][:], er_start[0:EP, :].rearrange("(p j) o -> p (j o)", p=P)[:, bass.ds(at, L)]).then_inc(loaded[s], 16)
                            sp.dma_start(idx[s][:], src[:, bass.ds(at, L)]).then_inc(loaded[s], 16)

                @block.gpsimd
                def _(pool):
                    if kind == "att":
                        pool.wait_ge(key_loaded, 16)
                        pool.indirect_dma_start(out=er_first[:], out_offset=None, in_=er_table,
                                                in_offset=bass.IndirectOffsetOnAxis(ap=key_first[:, 0:1], axis=0)
                                                ).then_inc(er_fetched, 16)
                    with pool.Fori(0, NCH // 2) as i:
                        for s in range(2):
                            if kind == "rel":
                                pool.wait_ge(idx_ready, 2 * i + s + 1)
                            else:
                                pool.wait_ge(loaded[s], 64 * i + 64)
                            pool.wait_ge(scanned, 2 * i + s + PRIMED - 1)
                            pool.sem_inc(issuing, 1)
                            for j in range(L):
                                pool.indirect_dma_start(
                                    out=G[s][:, j, :], out_offset=None, in_=table,
                                    in_offset=bass.IndirectOffsetOnAxis(ap=idx[s][:, j:j + 1], axis=0)
                                ).then_inc(gathered[s], 16)

                @block.vector
                def _(dve):
                    v = nc.vector
                    v.memset(S[1][:, L - 1, :], 0.0).then_inc(scanned, 1)
                    if kind == "att":
                        v.memset(top[1][:, L:L + 1], LOW).then_inc(scanned, 1)
                        dve.wait_ge(er_fetched, 16)
                        v.tensor_copy(er[1][:, L - 1:L], er_first[:]).then_inc(scanned, 1)
                    else:
                        v.memset(S[0][:, L - 1, :], 0.0).then_inc(scanned, 1)
                    if kind == "wsum":
                        v.memset(zero_b[:], 0.0).then_inc(zeroed, 1)
                    with dve.Fori(0, NCH // 2) as i:
                        for s in range(2):
                            k = 2 * i + s
                            dve.wait_ge(loaded[s], 64 * i + 64)
                            v.tensor_tensor(same[s][:], keys[s][:, 1:L + 1], keys[s][:, 0:L], ALU.is_equal).then_inc(same_ready, 1)
                            if kind == "rel":
                                v.scalar_tensor_tensor(idx[s][:], ty[s][:], float(NP), idx[s][:], ALU.mult, ALU.add).then_inc(idx_ready, 1)
                            if kind == "wsum":
                                for m, (what, t) in enumerate(((idx[s][:], 0), (keys[s][:, 1:L + 1], 1))):
                                    v.tensor_scalar(parts_i[:, 2 * m, :], what, 127, None, ALU.bitwise_and)
                                    last = v.tensor_scalar(parts_i[:, 2 * m + 1, :], what, 7, None, ALU.logical_shift_right)
                                last.then_inc(split, 1)
                                dve.wait_ge(split, k + 1)
                                v.tensor_copy(parts[:], parts_i[:]).then_inc(floated, 1)
                                dve.wait_ge(floated, k + 1)
                                for g in range(4):
                                    m, half, slot = g // 2, g % 2, g % 2
                                    dve.wait_ge(oh_used, 4 * k + g + 1)
                                    for j in range(HL):
                                        col = half * HL + j
                                        v.tensor_scalar(OH[:, slot, 0, j, :], iota_b[:], parts[:, 2 * m, col:col + 1], None, ALU.is_equal)
                                        last = v.tensor_scalar(OH[:, slot, 1, j, 0:HT], iota_b[:, 0:HT], parts[:, 2 * m + 1, col:col + 1], None, ALU.is_equal)
                                    last.then_inc(oh_ready, 1)
                            dve.wait_ge(gathered[s], 16 * L * (i + 1))
                            dve.wait_ge(stored[s], 16 * i)
                            dve.wait_ge(same_ready, k + 1)
                            if kind == "wsum":
                                v.tensor_tensor(G[s][:], G[s][:], wt[s][:].unsqueeze(2).to_broadcast([P, L, D]), ALU.mult).then_inc(weighed, 1)
                                dve.wait_ge(weighed, k + 1)
                            dve.wait_ge(scanned, k + PRIMED)
                            keep = same[s]
                            if kind == "att":
                                v.tensor_tensor_scan(er[s][:], same[s][:], er_in[s][:], er[1 - s][:, L - 1:L], ALU.mult, ALU.add)
                                v.tensor_scalar(cut[s][:], same[s][:], -LOW, LOW, ALU.mult, ALU.add)
                                v.tensor_copy(top[s][:, 0:1], top[1 - s][:, L:L + 1]).then_inc(att_step, 1)
                                dve.wait_ge(att_step, 5 * k + 1)
                                v.tensor_tensor(held[s][:], G[s][:, :, D], er[s][:], ALU.add).then_inc(att_step, 1)
                                dve.wait_ge(att_step, 5 * k + 2)
                                v.scalar_tensor_tensor(score[s][:], held[s][:], 0.2, held[s][:], ALU.mult, ALU.max).then_inc(att_step, 1)
                                dve.wait_ge(att_step, 5 * k + 3)
                                v.tensor_tensor_scan(top[s][:, 1:L + 1], cut[s][:], score[s][:], top[s][:, 0:1], ALU.add, ALU.max).then_inc(att_step, 1)
                                dve.wait_ge(att_step, 5 * k + 4)
                                v.tensor_tensor(held[s][:], top[s][:, 0:L], cut[s][:], ALU.add).then_inc(att_step, 1)
                                dve.wait_ge(att_step, 5 * k + 5)
                                v.tensor_tensor(ex[s][:, 0, :], held[s][:], top[s][:, 1:L + 1], ALU.subtract)
                                v.tensor_tensor(ex[s][:, 1, :], score[s][:], top[s][:, 1:L + 1], ALU.subtract)
                                v.tensor_copy(S[s][:, :, D + 1], top[s][:, 1:L + 1]).then_inc(ex_ready, 1)
                                dve.wait_ge(exped, k + 1)
                                v.tensor_tensor(G[s][:, :, 0:D], G[s][:, :, 0:D], ex[s][:, 1, :].unsqueeze(2).to_broadcast([P, L, D]), ALU.mult).then_inc(ex_ready, 1)
                                dve.wait_ge(ex_ready, 2 * k + 2)
                                v.tensor_tensor_scan(S[s][:, :, D], ex[s][:, 0, :], ex[s][:, 1, :], S[1 - s][:, L - 1, D:D + 1], ALU.mult, ALU.add)
                            for f in range(D):
                                last = v.tensor_tensor_scan(
                                    S[s][:, :, f], ex[s][:, 0, :] if kind == "att" else keep[:], G[s][:, :, f],
                                    S[1 - s][:, L - 1, f:f + 1], ALU.mult, ALU.add)
                            last.then_inc(scanned, 1)
                    if kind == "wsum":
                        dve.wait_ge(counted, 1)
                        v.tensor_copy(count_src[:], C[0][:, 0:HT])
                        v.tensor_copy(count_dst[:], C[1][:, 0:HT])

                @block.scalar
                def _(act):
                    with act.Fori(0, NCH // 2) as i:
                        for s in range(2):
                            if kind == "att":
                                act.wait_ge(ex_ready, 4 * i + 2 * s + 1)
                                nc.scalar.activation(ex[s][:], ex[s][:], ACT.Exp).then_inc(exped, 1)
                            act.wait_ge(scanned, 2 * i + s + 1 + PRIMED)
                            act.dma_start(rows_out[0:EP, :].rearrange("(p j) f -> p j f", p=P)[:, bass.ds((2 * i + s) * L, L), :],
                                          S[s][:]).then_inc(stored[s], 16)
                    for s in range(2):
                        act.wait_ge(stored[s], 16 * (NCH // 2))

                if kind == "wsum":
                    @block.tensor
                    def _(pe):
                        pe.wait_ge(zeroed, 1)
                        for m in range(2):
                            nc.tensor.matmul(C[m][:, 0:HT], zero_b[:], zero_b[:, 0:HT], start=True, stop=False, skip_group_check=True)
                        for g in range(2):
                            pe.sem_inc(oh_used, 1)
                        with pe.Fori(0, NCH) as k:
                            for g in range(4):
                                pe.wait_ge(oh_ready, 4 * k + g + 1)
                                for j in range(HL):
                                    last = nc.tensor.matmul(C[g // 2][:, 0:HT], OH[:, g % 2, 0, j, :], OH[:, g % 2, 1, j, 0:HT],
                                                            start=False, stop=False, skip_group_check=True)
                                last.then_inc(oh_used, 1)
                        for m in range(2):
                            last = nc.tensor.matmul(C[m][:, 0:HT], zero_b[:], zero_b[:, 0:HT], start=False, stop=True, skip_group_check=True)
                        last.then_inc(counted, 1)

        def places():
            with ExitStack() as c:
                ones = sb("ones", [P, P], c=c)
                flag = sb("flag", [P, HT], c=c)
                tile_end = sb("tile_end", [P, HT], c=c)
                last_place = sb("last_place", [P, HT], c=c)
                within, total = ps("within", [P, 512], c=c), ps("total", [P, 512], c=c)
                s_ones, s_sum, s_steps = semaphore("ones_made", c), semaphore("prefix_ready", c), semaphore("place_steps", c)
                block = phase(c)

                @block.vector
                def _(dve):
                    v = nc.vector
                    steps = Steps(dve, s_steps)
                    v.memset(ones[:], 1.0).then_inc(s_ones, 1)
                    dve.wait_ge(s_ones, 1)
                    dve.wait_ge(s_sum, 1)
                    for n, (count, first, end) in enumerate(((count_src, first_src, end_src), (count_dst, first_dst, end_dst))):
                        at = n * HT
                        steps.done(v.tensor_tensor_scan(tile_end[:], ones[:, 0:HT], total[:, at:at + HT], 0.0, ALU.mult, ALU.add))
                        steps.done(v.tensor_tensor(tile_end[:], tile_end[:], total[:, at:at + HT], ALU.subtract))
                        steps.done(v.tensor_tensor(first[:], tile_end[:], within[:, at:at + HT], ALU.add))
                        steps.done(v.tensor_scalar(flag[:], count[:], 0.0, None, ALU.is_gt))
                        steps.done(v.tensor_tensor(last_place[:], first[:], count[:], ALU.add))
                        steps.done(v.tensor_scalar(last_place[:], last_place[:], -1.0 - EP, None, ALU.add))
                        steps.done(v.tensor_tensor(last_place[:], last_place[:], flag[:], ALU.mult))
                        steps.done(v.tensor_scalar(last_place[:], last_place[:], float(EP), None, ALU.add))
                        steps.done(v.tensor_copy(end[:], last_place[:]))
                    steps.done(v.tensor_scalar(first_src[:], first_src[:], 1.0, None, ALU.add))

                @block.tensor
                def _(pe):
                    pe.wait_ge(s_ones, 1)
                    for n, count in enumerate((count_src, count_dst)):
                        nc.tensor.matmul(within[:, n * HT:(n + 1) * HT], below_b[:], count[:], start=True, stop=True)
                        last = nc.tensor.matmul(total[:, n * HT:(n + 1) * HT], ones[:], count[:], start=True, stop=True)
                    last.then_inc(s_sum, 1)

        def scatter_by_source():
            with ExitStack() as c:
                def slots(name, shape, dt=F32, n=2):
                    return [sb(f"sort_{name}{s}", shape, dt, c) for s in range(n)]

                def sem(name):
                    return semaphore(f"sort_{name}", c)

                feat = slots("feat", [P, L, A])
                row = slots("row", [P, L, A + 1])
                keys = slots("keys", [P, L], I32)
                place = slots("place", [P, L])
                place_i = slots("place_i", [P, L], I32)
                parts_i = sb("sort_parts_i", [P, 2, L], I32, c)
                parts = sb("sort_parts", [P, 2, L], F32, c)
                low = slots("low", [P, P], BF16, 4)
                high = slots("high", [P, HT], BF16, 6)
                lowT = slots("lowT", [P, P], BF16)
                lowTf = slots("lowTf", [P, P])
                before = slots("before", [P, P], BF16, 4)
                counts = slots("counts", [P, HT])
                junk = slots("junk", [P, HT])
                ident_b = sb("ident_b", [P, P], BF16, c)
                pT = [ps(f"pT{s}", [P, 1024], BF16, c) for s in range(2)]
                pS = [ps(f"pS{s}", [P, 512], F32, c) for s in range(2)]
                pG = [ps(f"pG{s}", [P, 512], F32, c) for s in range(3)]
                pC = ps("pC", [P, 512], F32, c)
                loaded = [sem(f"loaded{s}") for s in range(2)]
                scattered = [semaphore(f"scattered{s}") for s in range(2)]
                (rows_ready, split, floated, onehot, turned, turned_copied, same_low, before_ready, summed,
                 counted, copied, placed, place_ready, started, issuing) = (
                    sem(n) for n in ("rows_ready", "split", "floated", "onehot", "turned", "turned_copied", "same_low",
                                     "before_ready", "summed", "counted", "copied", "placed", "place_ready", "started", "issuing"))
                block = phase(c)

                @block.sync
                def _(sp):
                    with sp.Fori(0, NCH // 2) as i:
                        for s in range(2):
                            at = (2 * i + s) * L
                            sp.wait_ge(rows_ready, 2 * i)
                            sp.wait_ge(floated, 2 * i)
                            sp.dma_start(keys[s][:], src[:, bass.ds(at, L)]).then_inc(loaded[s], 16)
                            sp.dma_start(feat[s][:], attr.rearrange("(p j) f -> p j f", p=P)[:, bass.ds(at, L), :]).then_inc(loaded[s], 16)

                @block.gpsimd
                def _(pool):
                    with pool.Fori(0, NCH // 2) as i:
                        for s in range(2):
                            pool.wait_ge(place_ready, 2 * i + s + 1)
                            pool.wait_ge(rows_ready, 2 * i + s + 1)
                            pool.sem_inc(issuing, 1)
                            for j in range(L):
                                pool.indirect_dma_start(
                                    out=by_src, out_offset=bass.IndirectOffsetOnAxis(ap=place_i[s][:, j:j + 1], axis=0),
                                    in_=row[s][:, j, :], in_offset=None).then_inc(scattered[s], 16)
                    for s in range(2):
                        pool.wait_ge(scattered[s], 16 * L * (NCH // 2))

                @block.vector
                def _(dve):
                    v = nc.vector
                    v.tensor_copy(ident_b[:], ident[:]).then_inc(started, 1)
                    v.tensor_copy(counts[0][:], first_src[:]).then_inc(copied, 1)
                    with dve.Fori(0, NCH // 2) as i:
                        for s in range(2):
                            k = 2 * i + s
                            dve.wait_ge(loaded[s], 32 * i + 32)
                            v.tensor_scalar(parts_i[:, 0, :], keys[s][:], 127, None, ALU.bitwise_and)
                            v.tensor_scalar(parts_i[:, 1, :], keys[s][:], 7, None, ALU.logical_shift_right).then_inc(split, 1)
                            dve.wait_ge(split, k + 1)
                            v.tensor_copy(parts[:], parts_i[:]).then_inc(floated, 1)
                            dve.wait_ge(floated, k + 1)
                            for q in range(L + 3):
                                if q < L:
                                    b = q % 4
                                    if q >= 6:
                                        dve.wait_ge(placed, k * L + q - 5)
                                    v.tensor_scalar(low[b][:], iota_b[:], parts[:, 0, q:q + 1], None, ALU.is_equal)
                                    v.tensor_scalar(high[q % 6][:], iota_b[:, 0:HT], parts[:, 1, q:q + 1], None, ALU.is_equal).then_inc(onehot, 1)
                                if 0 <= q - 2 < L:
                                    t, b = k * L + q - 2, (q - 2) % 4
                                    dve.wait_ge(same_low, t + 1)
                                    v.tensor_tensor(before[b][:], pS[b % 2][:, 0:P], below_b[:], ALU.mult).then_inc(before_ready, 1)
                                if 0 <= q - 3 < L:
                                    t = k * L + q - 3
                                    dve.wait_ge(summed, t + 1)
                                    if q - 3 >= 2:
                                        dve.wait_ge(placed, t - 1)
                                    v.tensor_tensor_reduce(out=junk[q % 2][:], in0=pG[(q - 3) % 3][:, 0:HT], in1=high[(q - 3) % 6][:], scale=1.0, scalar=0.0,
                                                           op0=ALU.mult, op1=ALU.add, accum_out=place[s][:, q - 3:q - 2]).then_inc(placed, 1)
                            dve.wait_ge(placed, k * L + L)
                            dve.wait_ge(scattered[s], 16 * L * i)
                            v.tensor_copy(place_i[s][:], place[s][:]).then_inc(place_ready, 1)

                @block.scalar
                def _(act):
                    a = nc.scalar
                    with act.Fori(0, NCH // 2) as i:
                        for s in range(2):
                            k = 2 * i + s
                            act.wait_ge(loaded[s], 32 * i + 32)
                            act.wait_ge(scattered[s], 16 * L * i)
                            a.copy(row[s][:, :, 0:A], feat[s][:])
                            a.copy(row[s][:, :, A], keys[s][:]).then_inc(rows_ready, 1)
                            for q in range(L + 1):
                                if q < L:
                                    t = k * L + q
                                    act.wait_ge(turned, t + 1)
                                    a.copy(lowT[q % 2][:], pT[q % 2][:, 0:P])
                                    a.copy(lowTf[q % 2][:], pT[q % 2][:, 0:P]).then_inc(turned_copied, 1)
                                if q >= 1:
                                    t = k * L + q - 1
                                    act.wait_ge(counted, t + 1)
                                    a.copy(counts[q % 2][:], pC[:, 0:HT]).then_inc(copied, 1)

                @block.tensor
                def _(pe):
                    mm = nc.tensor.matmul
                    pe.wait_ge(started, 1)
                    mm(pC[:, 0:HT], ident[:], first_src[:], start=True, stop=False, skip_group_check=True)
                    with pe.Fori(0, NCH // 2) as i:
                        for s in range(2):
                            k = 2 * i + s
                            for q in range(L + 2):
                                if q < L:
                                    pe.wait_ge(onehot, k * L + q + 1)
                                    nc.tensor.transpose(pT[q % 2][:, 0:P], low[q % 4][:], ident_b[:]).then_inc(turned, 1)
                                if 0 <= q - 1 < L:
                                    j, t = q - 1, k * L + q - 1
                                    pe.wait_ge(turned_copied, t + 1)
                                    mm(pS[j % 2][:, 0:P], lowT[j % 2][:], lowT[j % 2][:], start=True, stop=True).then_inc(same_low, 1)
                                    pe.wait_ge(copied, t + 1)
                                    if j >= 3:
                                        pe.wait_ge(placed, t - 2)
                                    mm(pG[j % 3][:, 0:HT], lowTf[j % 2][:], counts[j % 2][:], start=True, stop=False)
                                    mm(pC[:, 0:HT], low[j % 4][:], high[j % 6][:], start=False, stop=False,
                                       skip_group_check=True).then_inc(counted, 1)
                                if 0 <= q - 2 < L:
                                    j, t = q - 2, k * L + q - 2
                                    pe.wait_ge(before_ready, t + 1)
                                    mm(pG[j % 3][:, 0:HT], before[j % 4][:], high[j % 6][:], start=False, stop=True).then_inc(summed, 1)

        def pooled_layer():
            with ExitStack() as c:
                def slots(name, shape, dt=F32):
                    return [sb(f"pool_{name}{s}", shape, dt, c) for s in range(2)]

                row = slots("row", [P, L + 1, A + 1])
                S = slots("S", [P, L, 2 * A])
                same = slots("same", [P, L])
                cut = slots("cut", [P, L])
                loaded = [semaphore(f"pool_loaded{s}", c) for s in range(2)]
                stored = [semaphore(f"pool_stored{s}", c) for s in range(2)]
                same_ready, cut_ready, scanned = (semaphore(f"pool_{n}", c) for n in ("same_ready", "cut_ready", "scanned"))
                block = phase(c)
                rows = lambda off: by_src[off:EP + off, :].rearrange("(p j) f -> p j f", p=P)

                @block.sync
                def _(sp):
                    with sp.Fori(0, NCH // 2) as i:
                        for s in range(2):
                            at = (2 * i + s) * L
                            sp.wait_ge(scanned, 2 * i + s + 1)
                            sp.dma_start(row[s][:, 0:L, :], rows(0)[:, bass.ds(at, L), :]).then_inc(loaded[s], 16)
                            sp.dma_start(row[s][:, L:L + 1, :], rows(1)[:, bass.ds(at + L - 1, 1), :]).then_inc(loaded[s], 16)

                @block.vector
                def _(dve):
                    v = nc.vector
                    v.memset(S[1][:, L - 1, 0:A], 0.0).then_inc(scanned, 1)
                    v.memset(S[1][:, L - 1, A:], LOW).then_inc(scanned, 1)
                    with dve.Fori(0, NCH // 2) as i:
                        for s in range(2):
                            k = 2 * i + s
                            dve.wait_ge(loaded[s], 32 * i + 32)
                            v.tensor_tensor(same[s][:], row[s][:, 1:L + 1, A], row[s][:, 0:L, A], ALU.is_equal).then_inc(same_ready, 1)
                            dve.wait_ge(same_ready, k + 1)
                            v.tensor_scalar(cut[s][:], same[s][:], -LOW, LOW, ALU.mult, ALU.add).then_inc(cut_ready, 1)
                            dve.wait_ge(cut_ready, k + 1)
                            dve.wait_ge(stored[s], 16 * i)
                            dve.wait_ge(scanned, k + 2)
                            for f in range(2 * A):
                                top = f >= A
                                last = v.tensor_tensor_scan(
                                    S[s][:, :, f], (cut if top else same)[s][:], row[s][:, 1:L + 1, f % A], S[1 - s][:, L - 1, f:f + 1],
                                    ALU.add if top else ALU.mult, ALU.max if top else ALU.add)
                            last.then_inc(scanned, 1)

                @block.scalar
                def _(act):
                    with act.Fori(0, NCH // 2) as i:
                        for s in range(2):
                            act.wait_ge(scanned, 2 * i + s + 3)
                            act.dma_start(scan_pool[0:EP, :].rearrange("(p j) f -> p j f", p=P)[:, bass.ds((2 * i + s) * L, L), :],
                                          S[s][:]).then_inc(stored[s], 16)
                    for s in range(2):
                        act.wait_ge(stored[s], 16 * (NCH // 2))

        def fetch_nodes(kind, rows, end, F, V, K):
            with ExitStack() as c:
                key_t = F32 if kind == "pool" else I32
                edge_keys = sb(f"{kind}_edge_keys", [P, 4], key_t, c)
                ek = sb(f"{kind}_ek", [P, 4], F32, c)
                fl = sb(f"{kind}_fl", [P, 8], F32, c)
                tail = sb(f"{kind}_tail", [P, F], F32, c)
                tailT, contT, fullT, tmT = (sb(f"{kind}_{n}T", [F, P], F32, c) for n in ("tail", "cont", "full", "tm"))
                d0, d1, cinT, mc, tmp = (sb(f"{kind}_{n}", [F, P], F32, c) for n in ("d0", "d1", "cinT", "mc", "tmp"))
                cin = sb(f"{kind}_cin", [P, F + 1], F32, c)
                iota_g = sb(f"{kind}_iota_g", [P, TG * P], F32, c)
                sel = [sb(f"{kind}_sel{s}", [P, TG * P], F32, c) for s in range(2)]
                fk = sb(f"{kind}_fk", [P, NG], F32, c)
                pK = [ps(f"{kind}_pK{s}", [P, 512], c=c) for s in range(2)]
                pR = [ps(f"{kind}_pR{s}", [P, 512], c=c) for s in range(2)]
                s_keys, s_tail, s_iota, s_steps, s_flags, s_T, s_cinT, s_cinP, s_cin, s_sel, s_K, s_copied, s_e, s_exp = (
                    semaphore(f"{kind}_f_{n}", c) for n in
                    ("keys", "tail", "iota", "steps", "flags", "turned", "cinT", "cin_turned", "cin", "sel", "K", "copied", "expo", "exped"))
                block = phase(c)
                s_V = V_fetched[kind]
                if kind == "pool":
                    col = lambda off, at: by_src[off:EP + off, A:A + 1].rearrange("(p j) o -> p (j o)", p=P)[:, at:at + 1]
                else:
                    col = lambda off, at: dst[off:EP + off].rearrange("(p j) -> p j", p=P)[:, at:at + 1]

                @block.sync
                def _(sp):
                    sp.dma_start(edge_keys[:, 0:1], col(1, 0), allow_slow_non_contiguous=True).then_inc(s_keys, 16)
                    sp.dma_start(edge_keys[:, 1:2], col(0, 0), allow_slow_non_contiguous=True).then_inc(s_keys, 16)
                    sp.dma_start(edge_keys[:, 2:3], col(1, J - 1), allow_slow_non_contiguous=True).then_inc(s_keys, 16)
                    sp.dma_start(edge_keys[:, 3:4], col(2, J - 1), allow_slow_non_contiguous=True).then_inc(s_keys, 16)
                    sp.dma_start(tail[:], rows[0:EP, :].rearrange("(p j) f -> p j f", p=P)[:, J - 1, :]).then_inc(s_tail, 16)

                @block.gpsimd
                def _(pool):
                    nc.gpsimd.iota(iota_g[:], [[1, TG * P]], base=0, channel_multiplier=0,
                                   allow_small_or_imprecise_dtypes=True).then_inc(s_iota, 1)
                    for h in range(HT):
                        pool.indirect_dma_start(out=V[:, h, :], out_offset=None, in_=rows,
                                                in_offset=bass.IndirectOffsetOnAxis(ap=end[:, h:h + 1], axis=0)).then_inc(s_V, 16)
                    pool.wait_ge(s_V, 16 * HT)

                @block.vector
                def _(dve):
                    v = nc.vector
                    st = Steps(dve, s_steps)
                    dve.wait_ge(s_keys, 64)
                    st.done(v.tensor_copy(ek[:], edge_keys[:]))
                    cont, full, contn, valid = (fl[:, n:n + 1] for n in range(4))
                    v.tensor_tensor(cont, ek[:, 0:1], ek[:, 1:2], ALU.is_equal)
                    v.tensor_tensor(full, ek[:, 0:1], ek[:, 2:3], ALU.is_equal)
                    st.done(v.tensor_tensor(contn, ek[:, 2:3], ek[:, 3:4], ALU.is_equal))
                    st.done(v.tensor_tensor(valid, full, contn, ALU.mult))
                    st.done(v.tensor_scalar(valid, valid, -1.0, 1.0, ALU.mult, ALU.add))
                    st.done(v.tensor_tensor(valid, valid, cont, ALU.mult))
                    st.done(v.tensor_scalar(fl[:, 4:5], ek[:, 0:1], 1.0, None, ALU.add))
                    st.done(v.tensor_tensor(fl[:, 4:5], fl[:, 4:5], valid, ALU.mult))
                    for g in range(NG):
                        last = v.tensor_scalar(fk[:, g:g + 1], fl[:, 4:5], -1.0 - g * TG * P, None, ALU.add)
                    last.then_inc(s_flags, 1)
                    dve.wait_ge(s_T, 1)
                    v.tensor_copy(tailT[:], pR[0][0:F, 0:P])
                    v.tensor_copy(contT[:], pR[1][0:F, 0:P])
                    if kind == "att":
                        v.tensor_copy(tmT[:], pR[1][0:F, 2 * P:3 * P])
                    st.done(v.tensor_copy(fullT[:], pR[1][0:F, P:2 * P]))
                    c1, f1, t1 = contT[:, 1:P], fullT[:, 0:P - 1], tailT[:, 0:P - 1]
                    v.memset(d0[:, 0:1], 0.0)
                    v.memset(d1[:, 0:1], 0.0)
                    st.done(v.tensor_tensor(d0[:, 1:P], c1, f1, ALU.mult))
                    if kind == "att":
                        m1 = tmT[:, 0:P - 1]
                        v.memset(cinT[:, 0:1], LOW)
                        v.memset(tmp[:, 0:1], LOW)
                        st.done(v.tensor_scalar(cinT[:, 1:P], c1, -LOW, LOW, ALU.mult, ALU.add))
                        st.done(v.tensor_scalar(tmp[:, 1:P], d0[:, 1:P], -LOW, LOW, ALU.mult, ALU.add))
                        st.done(v.tensor_tensor(d1[:, 1:P], m1, c1, ALU.mult))
                        st.done(v.tensor_tensor(cinT[:, 1:P], cinT[:, 1:P], d1[:, 1:P], ALU.add))
                        st.done(v.tensor_tensor_scan(mc[:], tmp[:], cinT[:], LOW, ALU.add, ALU.max))
                        v.memset(tmp[:, 0:1], 0.0)
                        st.done(v.tensor_tensor(tmp[:, 1:P], mc[:, 0:P - 1], mc[:, 1:P], ALU.subtract))
                        st.done(v.tensor_scalar(tmp[:], tmp[:], 0.0, None, ALU.min))
                        v.tensor_tensor(d1[:, 1:P], m1, mc[:, 1:P], ALU.subtract).then_inc(s_e, 1)
                        dve.wait_ge(s_e, 1)
                        v.tensor_scalar(d1[:], d1[:], 0.0, None, ALU.min).then_inc(s_e, 1)
                        dve.wait_ge(s_exp, 1)
                        st.done(v.tensor_tensor(d0[:], d0[:], tmp[:], ALU.mult))
                        st.done(v.tensor_tensor(d1[:, 1:P], d1[:, 1:P], c1, ALU.mult))
                        st.done(v.tensor_tensor(d1[:, 1:P], d1[:, 1:P], t1, ALU.mult))
                        st.done(v.memset(d1[:, 0:1], 0.0))
                    else:
                        st.done(v.tensor_tensor(d1[:, 1:P], t1, c1, ALU.mult))
                    if kind == "pool":
                        st.done(v.tensor_tensor_scan(cinT[0:A, :], d0[0:A, :], d1[0:A, :], 0.0, ALU.mult, ALU.add))
                        v.memset(mc[A:F, 0:1], LOW)
                        v.memset(tmp[A:F, 0:1], LOW)
                        st.done(v.tensor_scalar(mc[A:F, 1:P], contT[A:F, 1:P], -LOW, LOW, ALU.mult, ALU.add))
                        st.done(v.tensor_tensor(mc[A:F, 1:P], mc[A:F, 1:P], d1[A:F, 1:P], ALU.add))
                        st.done(v.tensor_scalar(tmp[A:F, 1:P], d0[A:F, 1:P], -LOW, LOW, ALU.mult, ALU.add))
                        v.tensor_tensor_scan(cinT[A:F, :], tmp[A:F, :], mc[A:F, :], LOW, ALU.add, ALU.max).then_inc(s_cinT, 1)
                    else:
                        v.tensor_tensor_scan(cinT[:], d0[:], d1[:], 0.0, ALU.mult, ALU.add).then_inc(s_cinT, 1)
                    dve.wait_ge(s_cinP, 1)
                    if kind == "att":
                        v.tensor_copy(cin[:, F - 1:F], pR[1][:, 0:1])
                        v.tensor_copy(cin[:, 0:F - 1], pR[0][:, 0:F - 1])
                    else:
                        v.tensor_copy(cin[:, 0:F], pR[0][:, 0:F])
                    v.memset(cin[:, F:F + 1], 1.0).then_inc(s_cin, 1)
                    dve.wait_ge(s_iota, 1)
                    st.done(v.engine_nop()) if False else None
                    dve.wait_ge(s_flags, 1)
                    for g in range(NG):
                        if g >= 2:
                            dve.wait_ge(s_K, g - 1)
                        v.tensor_scalar(sel[g % 2][:], iota_g[:], fk[:, g:g + 1], None, ALU.is_equal).then_inc(s_sel, 1)

                @block.scalar
                def _(act):
                    if kind == "att":
                        act.wait_ge(s_e, 2)
                        nc.scalar.activation(tmp[:], tmp[:], ACT.Exp)
                        nc.scalar.activation(d1[:, 1:P], d1[:, 1:P], ACT.Exp).then_inc(s_exp, 1)
                    for g in range(NG):
                        act.wait_ge(s_K, g + 1)
                        nc.scalar.copy(K[:, g * TG:(g + 1) * TG, :],
                                       pK[g % 2][:, 0:TG * (F + 1)].rearrange("p (t f) -> p t f", t=TG)).then_inc(s_copied, 1)

                @block.tensor
                def _(pe):
                    mm = nc.tensor.matmul
                    pe.wait_ge(s_tail, 16)
                    pe.wait_ge(s_flags, 1)
                    mm(pR[0][0:F, 0:P], tail[:], ident[:], start=True, stop=True)
                    if kind == "att":
                        mm(pR[1][0:F, 2 * P:3 * P], tail[:, F - 1:F].to_broadcast([P, F]), ident[:], start=True, stop=True)
                    mm(pR[1][0:F, P:2 * P], fl[:, 1:2].to_broadcast([P, F]), ident[:], start=True, stop=True)
                    mm(pR[1][0:F, 0:P], fl[:, 0:1].to_broadcast([P, F]), ident[:], start=True, stop=True).then_inc(s_T, 1)
                    pe.wait_ge(s_cinT, 1)
                    if kind == "att":
                        mm(pR[1][:, 0:F], mc[:], ident[0:F, 0:F], start=True, stop=True)
                    mm(pR[0][:, 0:F], cinT[:], ident[0:F, 0:F], start=True, stop=True).then_inc(s_cinP, 1)
                    pe.wait_ge(s_cin, 1)
                    for g in range(NG):
                        pe.wait_ge(s_sel, g + 1)
                        if g >= 2:
                            pe.wait_ge(s_copied, g - 1)
                        for t in range(TG):
                            last = mm(pK[g % 2][:, t * (F + 1):(t + 1) * (F + 1)], sel[g % 2][:, t * P:(t + 1) * P], cin[:], start=True, stop=True)
                        last.then_inc(s_K, 1)

        def project(kind, V, K, V3=None):
            with ExitStack() as c:
                F = D if kind == "wsum" else 3 * A + 1
                w_in = sb(f"{kind}_w_in", [F, HID] if kind == "pool" else [D, D], F32, c)
                w_out = sb(f"{kind}_w_out", [HID if kind == "pool" else D, D], F32, c)
                bias = sb(f"{kind}_bias", [P, D], F32, c)
                b_hid = sb(f"{kind}_b_hid", [P, 1], F32, c)
                u_b = sb(f"{kind}_u_b", [P, 1], F32, c)
                VT = [sb(f"{kind}_VT{s}", [F, TG * P], F32, c) for s in range(2)]
                hid = [sb(f"{kind}_hid{s}", [P, TG * P], F32, c) for s in range(2)]
                pV = ps(f"{kind}_pV", [P, 1024], c=c)
                pH = ps(f"{kind}_pH", [P, 1024], c=c)
                pO = [ps(f"{kind}_pO{s}", [P, 512], c=c) for s in range(2)]
                s_w, s_wt, s_wT, s_steps, s_rows, s_turned, s_VT, s_hidP, s_hid, s_out, s_added = (
                    semaphore(f"{kind}_p_{n}", c) for n in
                    ("weights", "w_turned", "w_ready", "steps", "rows", "turned", "VT", "hidden", "hidden_ready", "out", "added"))
                block = phase(c)
                rowsV = V if kind == "wsum" else V3
                NW = 32 if kind == "wsum" else 80

                @block.sync
                def _(sp):
                    if kind == "wsum":
                        sp.dma_start(w_in[:], W0).then_inc(s_w, 16)
                        sp.dma_start(bias[:], b0.unsqueeze(0).to_broadcast([P, D])).then_inc(s_w, 16)
                    else:
                        sp.dma_start(w_in[:], W1).then_inc(s_w, 16)
                        sp.dma_start(w_out[:], W2).then_inc(s_w, 16)
                        sp.dma_start(bias[:], b2.unsqueeze(0).to_broadcast([P, D])).then_inc(s_w, 16)
                        sp.dma_start(b_hid[:], b1.unsqueeze(1), allow_slow_non_contiguous=True).then_inc(s_w, 16)
                        sp.dma_start(u_b[:], u[0:1, 0:1].to_broadcast([P, 1]), allow_slow_non_contiguous=True).then_inc(s_w, 16)

                @block.vector
                def _(dve):
                    v = nc.vector
                    st = Steps(dve, s_steps)
                    dve.wait_ge(s_w, NW)
                    if kind == "wsum":
                        v.tensor_tensor(V[:], V[:], K[:, :, 0:D], ALU.add).then_inc(s_rows, 1)
                        dve.wait_ge(s_wt, 1)
                        v.tensor_copy(w_out[:], pH[0:D, 0:D]).then_inc(s_wT, 1)
                    else:
                        count = stat[:, 0, :]
                        wide = lambda a, n: a.unsqueeze(2).to_broadcast([P, HT, n])
                        v.tensor_tensor(V3[:, :, 0:A], V[:, :, 0:A], K[:, :, 0:A], ALU.add)
                        st.done(v.tensor_scalar(count, count_src[:], 1.0, None, ALU.max))
                        st.done(v.reciprocal(count, count))
                        v.tensor_tensor(V3[:, :, 2 * A:3 * A], V3[:, :, 0:A], wide(count, A), ALU.mult)
                        st.done(v.tensor_scalar(stat[:, 1, :], K[:, :, D], -LOW, LOW, ALU.mult, ALU.add))
                        st.done(v.tensor_tensor(K[:, :, A:D], K[:, :, A:D], wide(stat[:, 1, :], A), ALU.add))
                        v.tensor_tensor(V3[:, :, A:2 * A], V[:, :, A:D], K[:, :, A:D], ALU.max)
                        v.tensor_copy(V3[:, :, 3 * A:3 * A + 1], u_b[:].unsqueeze(1).to_broadcast([P, HT, 1])).then_inc(s_rows, 1)
                    st.done(v.tensor_tensor(X[:], X[:], bias[:].unsqueeze(1).to_broadcast([P, HT, D]), ALU.add))
                    with dve.Fori(0, NG // 2) as i:
                        for s in range(2):
                            g = 2 * i + s
                            dve.wait_ge(s_out, g + 1)
                            xg = X[:, bass.ds(g * TG, TG), :]
                            v.tensor_tensor(xg, xg, pO[s][:, 0:TG * D].rearrange("p (t d) -> p t d", t=TG), ALU.add).then_inc(s_added, 1)

                @block.scalar
                def _(act):
                    with act.Fori(0, NG // 2) as i:
                        for s in range(2):
                            g = 2 * i + s
                            act.wait_ge(s_turned, g + 1)
                            nc.scalar.copy(VT[s][:], pV[0:F, 0:TG * P]).then_inc(s_VT, 1)
                            if kind == "pool":
                                act.wait_ge(s_hidP, g + 1)
                                nc.scalar.activation(hid[s][:], pH[:, 0:TG * P], ACT.Relu, bias=b_hid[:, 0:1]).then_inc(s_hid, 1)

                @block.tensor
                def _(pe):
                    mm = nc.tensor.matmul
                    pe.wait_ge(s_w, NW)
                    if kind == "wsum":
                        nc.tensor.transpose(pH[0:D, 0:D], w_in[:], ident[0:D, 0:D]).then_inc(s_wt, 1)
                        pe.wait_ge(s_wT, 1)
                    pe.wait_ge(s_rows, 1)
                    for i in range(NG // 2):
                        for s in range(2):
                            g = 2 * i + s
                            for t in range(TG):
                                last = nc.tensor.transpose(pV[0:F, t * P:(t + 1) * P],
                                                           rowsV[:, g * TG + t, 0:F], ident[:])
                            last.then_inc(s_turned, 1)
                            pe.wait_ge(s_VT, g + 1)
                            left, w = VT[s], w_out
                            if kind == "pool":
                                mm(pH[:, 0:512], w_in[:], VT[s][:, 0:512], start=True, stop=True)
                                mm(pH[:, 512:TG * P], w_in[:], VT[s][:, 512:TG * P], start=True, stop=True).then_inc(s_hidP, 1)
                                pe.wait_ge(s_hid, g + 1)
                                left = hid[s]
                            if s == 0:
                                pe.wait_ge(s_added, 2 * i)
                            for t in range(TG):
                                last = mm(pO[s][:, t * D:(t + 1) * D], left[:, t * P:(t + 1) * P], w[:], start=True, stop=True)
                            last.then_inc(s_out, 1)

        def relation_table(scratch):
            with ExitStack() as c:
                wr = sb("wr", [D, R, D], F32, c)
                HTt = [sb(f"HT{s}", [D, P], F32, c) for s in range(2)]
                made = [sb(f"made{s}", [P, R, D], F32, c) for s in range(2)]
                pV = [ps(f"rel_pV{s}", [P, 512], c=c) for s in range(2)]
                pW = [ps(f"rel_pW{s}", [P, 512], c=c) for s in range(2)]
                s_w, s_steps, s_var, s_root, s_h, s_turned, s_HT, s_prod, s_made = (
                    semaphore(f"rt_{n}", c) for n in ("weights", "steps", "var", "root", "h", "turned", "HT", "prod", "made"))
                s_stored = [semaphore(f"rt_stored{s}", c) for s in range(2)]
                block = phase(c)

                @block.sync
                def _(sp):
                    sp.dma_start(wr[:], Wr.rearrange("r d f -> d r f")).then_inc(s_w, 16)
                    with sp.Fori(0, HT // 2) as i:
                        for s in range(2):
                            sp.wait_ge(s_made, 2 * i + s + 1)
                            sp.dma_start(rel_table.rearrange("(r n) d -> n r d", r=R)[bass.ds((2 * i + s) * P, P), :, :],
                                         made[s][:]).then_inc(s_stored[s], 16)
                    for s in range(2):
                        sp.wait_ge(s_stored[s], 16 * (HT // 2))

                @block.vector
                def _(dve):
                    steps = Steps(dve, s_steps)
                    vector_norm(dve, steps, scratch, s_var, s_root).then_inc(s_h, 1)
                    with dve.Fori(0, HT // 2) as i:
                        for s in range(2):
                            dve.wait_ge(s_turned, 2 * i + s + 1)
                            nc.vector.tensor_copy(HTt[s][:], pV[s][0:D, 0:P]).then_inc(s_HT, 1)

                @block.scalar
                def _(act):
                    scalar_norm(act, s_var, s_root)
                    with act.Fori(0, HT // 2) as i:
                        for s in range(2):
                            act.wait_ge(s_prod, 2 * i + s + 1)
                            act.wait_ge(s_stored[s], 16 * i)
                            nc.scalar.copy(made[s][:], pW[s][:].rearrange("p (r f) -> p r f", r=R)).then_inc(s_made, 1)

                @block.tensor
                def _(pe):
                    pe.wait_ge(s_w, 16)
                    pe.wait_ge(s_h, 1)
                    for i in range(HT // 2):
                        for s in range(2):
                            h = 2 * i + s
                            nc.tensor.transpose(pV[s][0:D, 0:P], H[:, h, :], ident[:]).then_inc(s_turned, 1)
                            pe.wait_ge(s_HT, h + 1)
                            if s == 0:
                                pe.wait_ge(s_made, 2 * i)
                            nc.tensor.matmul(pW[s][:], HTt[s][:], wr[:].rearrange("d r f -> d (r f)"), start=True, stop=True).then_inc(s_prod, 1)

        def relation_update(V, K, scratch):
            with ExitStack() as c:
                al, ar = (sb(n, [P, D], F32, c) for n in ("al", "ar"))
                zt = sb("zt", [P, HT, D + 1], F32, c)
                er = sb("er_nodes", [P, HT], F32, c)
                at_f = sb("at_f", [P, HT], F32, c)
                at_i = sb("at_i", [P, HT], I32, c)
                node = sb("node", [P, HT], F32, c)
                s_w, s_node, s_steps, s_var, s_root, s_table, s_er, s_stored = (
                    semaphore(f"ru_{n}", c) for n in ("weights", "node", "steps", "var", "root", "table", "er", "stored"))
                s_spread = semaphore("er_spread")
                block = phase(c)

                @block.sync
                def _(sp):
                    sp.dma_start(al[:], attn_l.unsqueeze(0).to_broadcast([P, D])).then_inc(s_w, 16)
                    sp.dma_start(ar[:], attn_r.unsqueeze(0).to_broadcast([P, D])).then_inc(s_w, 16)
                    sp.wait_ge(s_er, 1)
                    sp.dma_start(er_table.rearrange("(h p) o -> p (h o)", p=P), er[:], allow_slow_non_contiguous=True).then_inc(s_stored, 16)
                    sp.wait_ge(s_table, 1)
                    sp.dma_start(att_table.rearrange("(h p) d -> p h d", p=P), zt[:]).then_inc(s_stored, 16)
                    sp.wait_ge(s_stored, 32)

                @block.gpsimd
                def _(pool):
                    nc.gpsimd.iota(node[:], [[P, HT]], base=EP, channel_multiplier=1,
                                   allow_small_or_imprecise_dtypes=True).then_inc(s_node, 1)
                    pool.wait_ge(s_er, 1)
                    for h in range(HT):
                        pool.indirect_dma_start(out=er_start, out_offset=bass.IndirectOffsetOnAxis(ap=at_i[:, h:h + 1], axis=0),
                                                in_=er[:, h:h + 1], in_offset=None).then_inc(s_spread, 16)
                    pool.wait_ge(s_spread, 16 * HT)

                @block.vector
                def _(dve):
                    v = nc.vector
                    st = Steps(dve, s_steps)
                    wide = lambda a: a.unsqueeze(2).to_broadcast([P, HT, D])
                    row = lambda a: a[:].unsqueeze(1).to_broadcast([P, HT, D])
                    deg, rdeg, has, none = (stat[:, n, :] for n in range(4))
                    st.done(v.tensor_tensor(V[:], V[:], K[:, :, 0:D], ALU.add))
                    st.done(v.tensor_scalar(deg, count_dst[:], 1.0, None, ALU.max))
                    st.done(v.reciprocal(rdeg, deg))
                    v.tensor_scalar(has, count_dst[:], 0.0, None, ALU.is_gt)
                    st.done(v.tensor_scalar(none, count_dst[:], 0.0, None, ALU.is_equal))
                    st.done(v.tensor_tensor(V[:], V[:], wide(rdeg), ALU.mult))
                    st.done(v.tensor_scalar(V[:], V[:], 0.8, None, ALU.mult))
                    st.done(v.scalar_tensor_tensor(V[:], H[:], 0.2, V[:], ALU.mult, ALU.add))
                    st.done(v.scalar_tensor_tensor(V[:], V[:], 0.0, wide(has), ALU.max, ALU.mult))
                    st.done(v.tensor_tensor(H[:], H[:], wide(none), ALU.mult))
                    st.done(v.tensor_tensor(X[:], X[:], V[:], ALU.add))
                    st.done(v.tensor_tensor(X[:], X[:], H[:], ALU.add))
                    dve.wait_ge(s_node, 1)
                    st.done(v.tensor_scalar(at_f[:], count_dst[:], 0.0, None, ALU.is_gt))
                    st.done(v.tensor_tensor(node[:], node[:], stat[:, 3, :], ALU.mult))
                    st.done(v.tensor_tensor(at_f[:], at_f[:], first_dst[:], ALU.mult))
                    st.done(v.tensor_tensor(at_f[:], at_f[:], node[:], ALU.add))
                    st.done(v.tensor_copy(at_i[:], at_f[:]))
                    st.done(vector_norm(dve, st, scratch, s_var, s_root))
                    dve.wait_ge(s_w, 32)
                    st.done(v.tensor_tensor(scratch, H[:], row(ar), ALU.mult))
                    v.tensor_reduce(er[:], scratch, AX, ALU.add).then_inc(s_er, 1)
                    dve.wait_ge(s_er, 1)
                    v.tensor_copy(zt[:, :, 0:D], H[:])
                    st.done(v.tensor_tensor(scratch, H[:], row(al), ALU.mult))
                    v.tensor_reduce(zt[:, :, D:D + 1], scratch, AX, ALU.add).then_inc(s_table, 1)

                @block.scalar
                def _(act):
                    scalar_norm(act, s_var, s_root)

        def attention_update(V, K):
            with ExitStack() as c:
                ea = sb("ea", [P, 2, HT], F32, c)
                s_steps, s_e, s_exp, s_m, s_em, s_x, s_out = (
                    semaphore(f"au_{n}", c) for n in ("steps", "expo", "exped", "neg", "neg_exped", "x", "out"))
                block = phase(c)
                full = (N // P) * P

                @block.vector
                def _(dve):
                    v = nc.vector
                    st = Steps(dve, s_steps)
                    wide = lambda a, n: a.unsqueeze(2).to_broadcast([P, HT, n])
                    m_own, m_in, has = V[:, :, D + 1], K[:, :, D + 1], K[:, :, D + 2]
                    mi, mx, den = (stat[:, n, :] for n in range(3))
                    st.done(v.tensor_scalar(mi, has, -LOW, LOW, ALU.mult, ALU.add))
                    st.done(v.tensor_tensor(mi, mi, m_in, ALU.add))
                    st.done(v.tensor_tensor(mx, mi, m_own, ALU.max))
                    v.tensor_tensor(ea[:, 0, :], m_own, mx, ALU.subtract)
                    v.tensor_tensor(ea[:, 1, :], mi, mx, ALU.subtract).then_inc(s_e, 1)
                    dve.wait_ge(s_exp, 1)
                    v.tensor_tensor(V[:, :, 0:D + 1], V[:, :, 0:D + 1], wide(ea[:, 0, :], D + 1), ALU.mult)
                    st.done(v.tensor_tensor(K[:, :, 0:D + 1], K[:, :, 0:D + 1], wide(ea[:, 1, :], D + 1), ALU.mult))
                    st.done(v.tensor_tensor(V[:, :, 0:D + 1], V[:, :, 0:D + 1], K[:, :, 0:D + 1], ALU.add))
                    st.done(v.tensor_scalar(den, V[:, :, D], 0.5, None, ALU.max))
                    st.done(v.reciprocal(den, den))
                    st.done(v.tensor_tensor(H[:], V[:, :, 0:D], wide(den, D), ALU.mult))
                    v.tensor_scalar(K[:, :, 0:D], H[:], 0.0, None, ALU.min).then_inc(s_m, 1)
                    st.done(v.scalar_tensor_tensor(X[:], H[:], 0.0, X[:], ALU.max, ALU.add))
                    dve.wait_ge(s_em, 1)
                    v.scalar_tensor_tensor(X[:], K[:, :, 0:D], -1.0, X[:], ALU.add, ALU.add).then_inc(s_x, 1)

                @block.scalar
                def _(act):
                    act.wait_ge(s_e, 1)
                    nc.scalar.activation(ea[:], ea[:], ACT.Exp).then_inc(s_exp, 1)
                    act.wait_ge(s_m, 1)
                    nc.scalar.activation(K[:, :, 0:D], K[:, :, 0:D], ACT.Exp).then_inc(s_em, 1)

                @block.sync
                def _(sp):
                    sp.wait_ge(s_x, 1)
                    sp.dma_start(out[0:full, :].rearrange("(h p) d -> p h d", p=P), X[:, 0:N // P, :]).then_inc(s_out, 16)
                    if N > full:
                        sp.dma_start(out[full:N, :], X[0:N - full, N // P, :]).then_inc(s_out, 16)
                    sp.wait_ge(s_out, 32 if N > full else 16)

        made_rows = []
        V_fetched = {kind: semaphore(f"{kind}_V_fetched") for kind in ("wsum", "pool", "rel", "att")}

        def node_rows(F):
            c = ExitStack()
            n = len(made_rows)
            made_rows.append(F)
            return c, sb(f"rows{n}", [P, HT, F], F32, c), sb(f"carried{n}", [P, HT, F + 1], F32, c)


        gathered_layer("wsum", h_table, D, scan_wsum)
        places()
        c, V, K = node_rows(D)
        with c:
            fetch_nodes("wsum", scan_wsum, end_dst, D, V, K)
            project("wsum", V, K)
        scatter_by_source()
        pooled_layer()
        c, V, K = node_rows(D)
        with c:
            V3 = c.enter_context(nc.sbuf_tensor("V3", [P, HT, 3 * A + 1], F32))
            fetch_nodes("pool", scan_pool, end_src, D, V, K)
            project("pool", V, K, V3)
            relation_table(V[:])
        gathered_layer("rel", rel_table, D, scan_rel)
        c, V, K = node_rows(D)
        with c:
            fetch_nodes("rel", scan_rel, end_dst, D, V, K)
            relation_update(V, K, V[:])
        gathered_layer("att", att_table, D + 1, scan_att)
        c, V, K = node_rows(FM)
        with c:
            fetch_nodes("att", scan_att, end_dst, FM, V, K)
            attention_update(V, K)


def kernel(x, src, dst, edge_attr_32, edge_type_8, edge_weight1, L0_gnn_W, L0_gnn_b, L1_gnn_u, L1_gnn_W1, L1_gnn_b1,
           L1_gnn_W2, L1_gnn_b2, L2_gnn_weight_r, L3_gnn_attn_l, L3_gnn_attn_r):
    import numpy as np
    import concourse.bacc as bacc
    from concourse.bass_utils import run_bass_kernel_spmd

    L = 60
    arrays, n = layout(np, L, x, src, dst, edge_attr_32, edge_type_8, edge_weight1)
    weights = dict(W0=L0_gnn_W, b0=L0_gnn_b, u=L1_gnn_u, W1=L1_gnn_W1, b1=L1_gnn_b1, W2=L1_gnn_W2, b2=L1_gnn_b2,
                   Wr=L2_gnn_weight_r, attn_l=L3_gnn_attn_l, attn_r=L3_gnn_attn_r)
    arrays.update({k: np.ascontiguousarray(v) for k, v in weights.items()})
    nc = bacc.Bacc("TRN2", target_bir_lowering=False, num_devices=1)
    ins = {k: nc.dram_tensor(f"in_{k}", v.shape, mybir.dt.from_np(v.dtype), kind="ExternalInput").ap() for k, v in arrays.items()}
    out = nc.dram_tensor("out", [n, D], F32, kind="ExternalOutput").ap()
    build(nc, out=out, L=L, **ins)
    r = run_bass_kernel_spmd(nc, [{f"in_{k}": v for k, v in arrays.items()}], core_ids=[0])
    return r.results[0]["out"]


def layout(np, L, x, src, dst, attr, etype, weight):
    n, e = x.shape[0], src.shape[0]
    rows = -(-(n + 1) // (14 * P)) * 14 * P
    J = 2 * L * -(-e // (2 * L * P))
    ep = P * J

    def padded(a, shape, fill, at=0):
        b = np.full(shape, fill, a.dtype)
        b[at:at + a.shape[0]] = a
        return b

    x, src, dst, attr, etype, weight = (np.asarray(a) for a in (x, src, dst, attr, etype, weight))
    keys = padded(dst, (ep + 2,), n, 1)
    keys[0], keys[ep + 1] = -1, -2
    return dict(
        x=padded(x, (rows, x.shape[1]), 0), src=padded(src, (ep,), n).reshape(P, J), dst=keys,
        etype=padded(etype, (ep,), 0).reshape(P, J), weight=padded(weight.reshape(e), (ep,), 0).reshape(P, J),
        attr=padded(attr, (ep, attr.shape[1]), 0)), n
```

```python
import concourse.bass as bass
from concourse import mybir
from contextlib import ExitStack

P = 128
D = 64
A = 32
HID = 128
LOW = -1.7e38
F32 = mybir.dt.float32
BF16 = mybir.dt.bfloat16
I32 = mybir.dt.int32
ALU = mybir.AluOpType
ACT = mybir.ActivationFunctionType
AX = mybir.AxisListType.X


class Steps:

    def __init__(self, engine, sem):
        self.engine, self.sem, self.count = engine, sem, 0

    def done(self, instruction):
        self.count += 1
        instruction.then_inc(self.sem, 1)
        self.engine.wait_ge(self.sem, self.count)


def build(nc, x, src, dst, etype, weight, attr, W0, b0, u, W1, b1, W2, b2, Wr, attn_l, attn_r, out, L):
    J = src.shape[1]
    NCH = J // L
    EP = P * J
    N = out.shape[0]
    HT = x.shape[0] // P
    NP = HT * P
    R = Wr.shape[0]
    TG = 7
    NG = HT // TG
    HL = L // 2
    FM = D + 2
    assert NCH % 6 == 0 and HT % TG == 0 and L % 2 == 0 and NP > N

    h_table = nc.dram_tensor("h_table", [NP, D], F32, kind="Internal").ap()
    rel_table = nc.dram_tensor("rel_table", [R * NP, D], F32, kind="Internal").ap()
    att_table = nc.dram_tensor("att_table", [NP, D + 1], F32, kind="Internal").ap()
    rel_index = nc.dram_tensor("rel_index", [P, J], I32, kind="Internal").ap()
    er_table = nc.dram_tensor("er_table", [NP, 1], F32, kind="Internal").ap()
    er_start = nc.dram_tensor("er_start", [EP + NP, 1], F32, kind="Internal").ap()
    scan_wsum = nc.dram_tensor("scan_wsum", [EP + 1, D], F32, kind="Internal").ap()
    scan_pool = nc.dram_tensor("scan_pool", [EP + 1, D], F32, kind="Internal").ap()
    scan_rel = nc.dram_tensor("scan_rel", [EP + 1, D], F32, kind="Internal").ap()
    scan_att = nc.dram_tensor("scan_att", [EP + 1, FM], F32, kind="Internal").ap()
    by_src = nc.dram_tensor("by_src", [EP + 2, A + 1], F32, kind="Internal").ap()

    ctx = ExitStack()
    with ctx:
        def sb(name, shape, dt=F32, c=ctx):
            return c.enter_context(nc.sbuf_tensor(name, shape, dt))

        def ps(name, shape, dt=F32, c=ctx):
            return c.enter_context(nc.psum_tensor(name, shape, dt))

        phase_sems = []

        def semaphore(name, c=None):
            if c is None:
                return ctx.enter_context(nc.semaphore(name))
            phase_sems.append(c.enter_context(nc.semaphore(name)))
            return phase_sems[-1]

        def clear_semaphores():
            used = list(phase_sems)
            phase_sems.clear()
            with nc.Block() as block:
                @block.sync
                def _(sp):
                    for s in used:
                        sp.sem_clear(s)

        def phase(c):
            c.callback(clear_semaphores)
            return c.enter_context(nc.Block())

        X = sb("X", [P, HT, D])
        H = sb("H", [P, HT, D])
        ident = sb("ident", [P, P])
        count_src = sb("count_src", [P, HT])
        count_dst = sb("count_dst", [P, HT])
        first_src = sb("first_src", [P, HT])
        first_dst = sb("first_dst", [P, HT])
        end_src = sb("end_src", [P, HT], I32)
        end_dst = sb("end_dst", [P, HT], I32)
        iota_b = sb("iota_b", [P, P], BF16)
        below_b = sb("below_b", [P, P], F32)
        stat = sb("stat", [P, 4, HT])
        wsum_state = sb("wsum_state", [P, D])
        zero_row = sb("zero_row", [1, FM])

        TP = 2 * TG
        NPC = HT // TP

        def tiles(a, g):
            return a[:, g * TG:(g + 1) * TG]

        def group_wide(a, g, n):
            return tiles(a, g).unsqueeze(2).to_broadcast([P, TG, n])

        class GroupNorm:

            def __init__(self, dve, st, square, s_var, s_root):
                self.dve, self.st, self.square, self.s_var, self.s_root = dve, st, square, s_var, s_root

            def centre(self, g):
                v, st, xg, hg = nc.vector, self.st, tiles(X, g), tiles(H, g)
                mean, var = tiles(stat[:, 0, :], g), tiles(stat[:, 1, :], g)
                st.done(v.tensor_reduce(mean, xg, AX, ALU.add))
                st.done(v.scalar_tensor_tensor(hg, mean.unsqueeze(2).to_broadcast([P, TG, D]), -1.0 / D, xg, ALU.mult, ALU.add))
                st.done(v.tensor_tensor(self.square[:], hg, hg, ALU.mult))
                st.done(v.tensor_reduce(var, self.square[:], AX, ALU.add))
                v.tensor_scalar(var, var, 1.0 / D, 1e-5, ALU.mult, ALU.add).then_inc(self.s_var, 1)

            def scale(self, g, into):
                root = tiles(stat[:, 2, :], g)
                self.dve.wait_ge(self.s_root, g + 1)
                self.st.done(nc.vector.reciprocal(root, root))
                return nc.vector.scalar_tensor_tensor(into, tiles(H, g), 0.0, root.unsqueeze(2).to_broadcast([P, TG, D]), ALU.max, ALU.mult)

        def group_root(act, g, s_var, s_root):
            act.wait_ge(s_var, g + 1)
            nc.scalar.activation(tiles(stat[:, 2, :], g), tiles(stat[:, 1, :], g), ACT.Sqrt).then_inc(s_root, 1)

        with ExitStack() as c:
            square = sb("square0", [P, TG, D], c=c)
            iota_i = sb("iota_i", [P, P], c=c)
            zeros = sb("zeros", [P, J], c=c)
            sentinel = sb("sentinel", [1, 2 * (A + 1)], c=c)
            types, sources = sb("types", [P, J], I32, c), sb("sources", [P, J], I32, c)
            s_types, s_index = semaphore("types_loaded", c), semaphore("index_ready", c)
            s_x = [semaphore(f"x_loaded{n}", c) for n in range(NPC)]
            s_made, s_filled, s_steps, s_var, s_root, s_h, s_table = (
                semaphore(n, c) for n in
                ("consts_made", "filled", "norm_steps", "var_ready", "root_ready", "h_ready", "table_stored"))
            block = phase(c)

            @block.gpsimd
            def _(pool):
                nc.gpsimd.iota(iota_i[:], [[1, P]], base=0, channel_multiplier=0,
                               allow_small_or_imprecise_dtypes=True).then_inc(s_made, 1)
                nc.gpsimd.memset(ident[:], 1.0).then_inc(s_made, 1)
                nc.gpsimd.memset(below_b[:], 1.0).then_inc(s_made, 1)
                pool.wait_ge(s_made, 3)
                nc.gpsimd.affine_select(out=ident[:], in_=ident[:], compare_op=ALU.is_equal, fill=0.0, base=0,
                                        pattern=[[1, P]], channel_multiplier=-1).then_inc(s_made, 1)
                nc.gpsimd.affine_select(out=below_b[:], in_=below_b[:], compare_op=ALU.is_gt, fill=0.0, base=0,
                                        pattern=[[1, P]], channel_multiplier=-1).then_inc(s_made, 1)

            @block.vector
            def _(dve):
                nc.vector.memset(zero_row[:], 0.0).then_inc(s_filled, 1)
                nc.vector.memset(zeros[:], 0.0).then_inc(s_filled, 1)
                nc.vector.memset(sentinel[:, 0:A + 1], -1.0).then_inc(s_filled, 1)
                nc.vector.memset(sentinel[:, A + 1:], -2.0).then_inc(s_filled, 1)
                steps = Steps(dve, s_steps)
                norm = GroupNorm(dve, steps, square, s_var, s_root)
                for g in range(NG + 1):
                    if g < NG:
                        dve.wait_ge(s_x[g // 2], 16)
                        norm.centre(g)
                    if g >= 1:
                        norm.scale(g - 1, tiles(H, g - 1)).then_inc(s_h, 1)
                dve.wait_ge(s_types, 32)
                nc.vector.scalar_tensor_tensor(types[:], sources[:], float(R), types[:], ALU.mult, ALU.add).then_inc(s_index, 1)
                dve.wait_ge(s_made, 5)
                nc.vector.tensor_copy(iota_b[:], iota_i[:])

            @block.scalar
            def _(act):
                act.dma_start(types[:], etype).then_inc(s_types, 16)
                act.dma_start(sources[:], src).then_inc(s_types, 16)
                for g in range(NG):
                    group_root(act, g, s_var, s_root)
                act.wait_ge(s_index, 1)
                act.dma_start(rel_index, types[:]).then_inc(s_table, 16)

            @block.sync
            def _(sp):
                piece = lambda a, n: a.rearrange("(h p) d -> p h d", p=P)[:, n * TP:(n + 1) * TP, :]
                for n in range(NPC):
                    sp.dma_start(X[:, n * TP:(n + 1) * TP, :], piece(x, n)).then_inc(s_x[n], 16)
                sp.wait_ge(s_filled, 4)
                for rows in (scan_wsum, scan_pool, scan_rel):
                    sp.dma_start(rows[EP:EP + 1, :], zero_row[0:1, 0:D]).then_inc(s_table, 16)
                sp.dma_start(scan_att[EP:EP + 1, :], zero_row[0:1, :]).then_inc(s_table, 16)
                sp.dma_start(er_start[0:EP, :].rearrange("(p j) o -> p (j o)", p=P), zeros[:]).then_inc(s_table, 16)
                sp.dma_start(by_src[0:1, :], sentinel[0:1, 0:A + 1]).then_inc(s_table, 16)
                sp.dma_start(by_src[EP + 1:EP + 2, :], sentinel[0:1, A + 1:]).then_inc(s_table, 16)
                for n in range(NPC):
                    sp.wait_ge(s_h, 2 * n + 2)
                    sp.dma_start(piece(h_table, n), H[:, n * TP:(n + 1) * TP, :]).then_inc(s_table, 16)
                sp.wait_ge(s_table, 16 * (7 + NPC + 1))

        def gathered_layer(kind, table, width, rows_out, c0, c1, counts=None, pooled=False, ahead=None):
            F = FM if kind == "att" else D
            NAME = f"{kind}{c0}"
            NL = 3 if kind == "rel" else 4
            NC = c1 - c0
            SIDE = J // NC
            HG = SIDE // HL
            with ExitStack() as c:
                def slots(name, shape, dt=F32):
                    return [sb(f"{NAME}_{name}{s}", shape, dt, c) for s in range(2)]

                def sem(name):
                    return semaphore(f"{NAME}_{name}", c)

                G = ([ahead["rows"], sb(f"{NAME}_G1", [P, L, width], F32, c)] if ahead else slots("G", [P, L, width]))
                S = slots("S", [P, L, F])
                idx = slots("idx", [P, L], I32)
                keys = slots("keys", [P, L + 1], I32)
                same = slots("same", [P, L])
                loaded = [sem(f"loaded{s}") for s in range(2)]
                gathered = [ahead["gathered"] if ahead and s == 0 else semaphore(f"{NAME}_gathered{s}") for s in range(2)]
                stored = [sem(f"stored{s}") for s in range(2)]
                same_ready, scanned, issuing = sem("same_ready"), sem("scanned"), sem("issuing")
                PRIMED = 3 if kind == "att" else 2
                if kind == "wsum":
                    wt = slots("wt", [P, L])
                    weighed = sem("weighed")
                if counts:
                    by, count = counts
                    side_keys = slots("side_keys", [P, SIDE], I32)
                    parts_i = sb(f"{NAME}_parts_i", [P, 2, SIDE], I32, c)
                    parts = sb(f"{NAME}_parts", [P, 2, SIDE], BF16, c)
                    low = slots("low", [P, HL, P], BF16)
                    high = slots("high", [P, HL, HT], BF16)
                    zero_b = sb(f"{NAME}_zero_b", [P, P], BF16, c)
                    C = ps(f"{NAME}_C", [P, 512], c=c)
                    side_loaded = [sem(f"side_loaded{s}") for s in range(2)]
                    split, parted, oh_ready, oh_used, zeroed, counted, taken = (
                        sem(n) for n in ("split", "parted", "onehot_ready", "onehot_used", "zeroed", "counted", "taken"))
                if pooled:
                    prow = sb("pool_row", [P, SIDE + 1, A + 1], F32, c)
                    pS = sb("pool_S", [P, SIDE, 2 * A], F32, c)
                    psame = sb("pool_same", [P, SIDE], F32, c)
                    pcut = sb("pool_cut", [P, SIDE], F32, c)
                    pstate = sb("pool_state", [P, 2 * A], F32, c)
                    prow_loaded, psame_ready, pcut_ready, pscanned, pstate_ready, pstored = (
                        sem(n) for n in ("prow_loaded", "psame_ready", "pcut_ready", "pscanned", "pstate_ready", "pstored"))
                if kind == "att":
                    er_in = slots("er_in", [P, L])
                    er = slots("er", [P, L])
                    cut = slots("cut", [P, L])
                    score = slots("score", [P, L])
                    top = slots("top", [P, L + 1])
                    held = slots("held", [P, L])
                    ex = slots("ex", [P, 2, L])
                    er_first = sb("er_first", [P, 1], F32, c)
                    key_first = sb("key_first", [P, 1], I32, c)
                    er_fetched, key_loaded = semaphore("er_fetched"), sem("key_loaded")
                    att_step, ex_ready, exped = sem("att_step"), sem("ex_ready"), sem("exped")
                block = phase(c)
                by_part = lambda flat: flat.rearrange("(p j) -> p j", p=P)
                key_cols = lambda off, at, n: by_part(dst[off:EP + off])[:, bass.ds(at, n)]
                sorted_rows = lambda off: by_src[off:EP + off, :].rearrange("(p j) f -> p j f", p=P)

                @block.sync
                def _(sp):
                    if kind == "att":
                        sp.dma_start(key_first[:], by_part(dst[1:1 + EP])[:, 0:1], allow_slow_non_contiguous=True).then_inc(key_loaded, 16)
                    with sp.Fori(0, NC // 2) as i:
                        for s in range(2):
                            at = (2 * i + (s + c0)) * L
                            sp.wait_ge(scanned, 2 * i + s + PRIMED - 1)
                            sp.dma_start(idx[s][:], (rel_index if kind == "rel" else src)[:, bass.ds(at, L)]).then_inc(loaded[s], 16)
                            sp.dma_start(keys[s][:, 0:L], key_cols(0, at, L)).then_inc(loaded[s], 16)
                            sp.dma_start(keys[s][:, L:L + 1], key_cols(1, at + L - 1, 1), allow_slow_non_contiguous=True).then_inc(loaded[s], 16)
                            if kind == "wsum":
                                sp.dma_start(wt[s][:], weight[:, bass.ds(at, L)]).then_inc(loaded[s], 16)
                            if kind == "att":
                                sp.dma_start(er_in[s][:], er_start[0:EP, :].rearrange("(p j) o -> p (j o)", p=P)[:, bass.ds(at, L)]).then_inc(loaded[s], 16)
                            side = (2 * i + s) * SIDE
                            if counts:
                                sp.wait_ge(parted, 2 * i + s + 1)
                                sp.dma_start(side_keys[s][:], src[:, bass.ds(side, SIDE)] if by == "src" else key_cols(1, side, SIDE)
                                             ).then_inc(side_loaded[s], 16)
                            if pooled:
                                sp.wait_ge(pscanned, 2 * i + s + 1)
                                sp.dma_start(prow[:, 0:SIDE, :], sorted_rows(0)[:, bass.ds(side, SIDE), :]).then_inc(prow_loaded, 16)
                                sp.dma_start(prow[:, SIDE:SIDE + 1, :], sorted_rows(1)[:, bass.ds(side + SIDE - 1, 1), :]).then_inc(prow_loaded, 16)

                @block.gpsimd
                def _(pool):
                    if kind == "att":
                        pool.wait_ge(key_loaded, 16)
                        pool.indirect_dma_start(out=er_first[:], out_offset=None, in_=er_table,
                                                in_offset=bass.IndirectOffsetOnAxis(ap=key_first[:, 0:1], axis=0)
                                                ).then_inc(er_fetched, 16)

                    def gather(i, s):
                        pool.wait_ge(loaded[s], 16 * NL * i + 16 * NL)
                        pool.wait_ge(scanned, 2 * i + s + PRIMED - 1)
                        pool.sem_inc(issuing, 1)
                        for j in range(L):
                            pool.indirect_dma_start(
                                out=G[s][:, j, :], out_offset=None, in_=table,
                                in_offset=bass.IndirectOffsetOnAxis(ap=idx[s][:, j:j + 1], axis=0)
                            ).then_inc(gathered[s], 16)

                    if ahead:
                        gather(0, 1)
                    with pool.Fori(1 if ahead else 0, NC // 2) as i:
                        for s in range(2):
                            gather(i, s)

                @block.vector
                def _(dve):
                    v = nc.vector

                    def count_side(i, s):
                        k = 2 * i + s
                        dve.wait_ge(side_loaded[s], 16 * i + 16)
                        v.tensor_scalar(parts_i[:, 0, :], side_keys[s][:], 127, None, ALU.bitwise_and)
                        v.tensor_scalar(parts_i[:, 1, :], side_keys[s][:], 7, None, ALU.logical_shift_right).then_inc(split, 1)
                        dve.wait_ge(split, k + 1)
                        v.tensor_copy(parts[:], parts_i[:]).then_inc(parted, 1)
                        dve.wait_ge(parted, k + 3)
                        for g in range(HG):
                            n, b = 2 * HG * i + s * HG + g, (s * HG + g) % 2
                            dve.wait_ge(oh_used, n + 1)
                            part = lambda m, w: parts[:, m, g * HL:(g + 1) * HL].unsqueeze(2).to_broadcast([P, HL, w])
                            iota = lambda w: iota_b[:, 0:w].unsqueeze(1).to_broadcast([P, HL, w])
                            v.tensor_tensor(low[b][:], iota(P), part(0, P), ALU.is_equal)
                            v.tensor_tensor(high[b][:], iota(HT), part(1, HT), ALU.is_equal).then_inc(oh_ready, 1)

                    def pool_side(i, s):
                        k = 2 * i + s
                        dve.wait_ge(prow_loaded, 32 * k + 32)
                        v.tensor_tensor(psame[:], prow[:, 1:SIDE + 1, A], prow[:, 0:SIDE, A], ALU.is_equal).then_inc(psame_ready, 1)
                        dve.wait_ge(psame_ready, k + 1)
                        v.tensor_scalar(pcut[:], psame[:], -LOW, LOW, ALU.mult, ALU.add).then_inc(pcut_ready, 1)
                        dve.wait_ge(pcut_ready, k + 1)
                        dve.wait_ge(pstored, 16 * k + 16)
                        dve.wait_ge(pstate_ready, k + 1)
                        for f in range(2 * A):
                            top_f = f >= A
                            last = v.tensor_tensor_scan(
                                pS[:, :, f], (pcut if top_f else psame)[:], prow[:, 1:SIDE + 1, f % A], pstate[:, f:f + 1],
                                ALU.add if top_f else ALU.mult, ALU.max if top_f else ALU.add)
                        last.then_inc(pscanned, 1)
                        dve.wait_ge(pscanned, k + 2)
                        v.tensor_copy(pstate[:], pS[:, SIDE - 1, :]).then_inc(pstate_ready, 1)

                    if c0 == 0:
                        v.memset(S[1][:, L - 1, :], 0.0).then_inc(scanned, 1)
                    else:
                        v.tensor_copy(S[1][:, L - 1, :], wsum_state[:]).then_inc(scanned, 1)
                    if kind == "att":
                        v.memset(top[1][:, L:L + 1], LOW).then_inc(scanned, 1)
                        dve.wait_ge(er_fetched, 16)
                        v.tensor_copy(er[1][:, L - 1:L], er_first[:]).then_inc(scanned, 1)
                    else:
                        v.memset(S[0][:, L - 1, :], 0.0).then_inc(scanned, 1)
                    if counts:
                        v.memset(zero_b[:], 0.0).then_inc(zeroed, 1)
                        dve.sem_inc(parted, 1)
                        dve.sem_inc(parted, 1)
                    if pooled:
                        v.memset(pstate[:, 0:A], 0.0)
                        v.memset(pstate[:, A:], LOW).then_inc(pstate_ready, 1)
                        dve.sem_inc(pscanned, 1)
                    with dve.Fori(0, NC // 2) as i:
                        for s in range(2):
                            k = 2 * i + s
                            if counts:
                                count_side(i, s)
                            if pooled:
                                pool_side(i, s)
                            dve.wait_ge(loaded[s], 16 * NL * i + 16 * NL)
                            v.tensor_tensor(same[s][:], keys[s][:, 1:L + 1], keys[s][:, 0:L], ALU.is_equal).then_inc(same_ready, 1)
                            dve.wait_ge(gathered[s], 16 * L * (i + 1))
                            dve.wait_ge(stored[s], 16 * i + 16)
                            dve.wait_ge(same_ready, k + 1)
                            if kind == "wsum":
                                v.tensor_tensor(G[s][:], G[s][:], wt[s][:].unsqueeze(2).to_broadcast([P, L, D]), ALU.mult).then_inc(weighed, 1)
                                dve.wait_ge(weighed, k + 1)
                            dve.wait_ge(scanned, k + PRIMED)
                            if kind == "att":
                                v.tensor_tensor_scan(er[s][:], same[s][:], er_in[s][:], er[1 - s][:, L - 1:L], ALU.mult, ALU.add)
                                v.tensor_scalar(cut[s][:], same[s][:], -LOW, LOW, ALU.mult, ALU.add)
                                v.tensor_copy(top[s][:, 0:1], top[1 - s][:, L:L + 1]).then_inc(att_step, 1)
                                dve.wait_ge(att_step, 5 * k + 1)
                                v.tensor_tensor(held[s][:], G[s][:, :, D], er[s][:], ALU.add).then_inc(att_step, 1)
                                dve.wait_ge(att_step, 5 * k + 2)
                                v.scalar_tensor_tensor(score[s][:], held[s][:], 0.2, held[s][:], ALU.mult, ALU.max).then_inc(att_step, 1)
                                dve.wait_ge(att_step, 5 * k + 3)
                                v.tensor_tensor_scan(top[s][:, 1:L + 1], cut[s][:], score[s][:], top[s][:, 0:1], ALU.add, ALU.max).then_inc(att_step, 1)
                                dve.wait_ge(att_step, 5 * k + 4)
                                v.tensor_tensor(held[s][:], top[s][:, 0:L], cut[s][:], ALU.add).then_inc(att_step, 1)
                                dve.wait_ge(att_step, 5 * k + 5)
                                v.tensor_tensor(ex[s][:, 0, :], held[s][:], top[s][:, 1:L + 1], ALU.subtract)
                                v.tensor_tensor(ex[s][:, 1, :], score[s][:], top[s][:, 1:L + 1], ALU.subtract)
                                v.tensor_copy(S[s][:, :, D + 1], top[s][:, 1:L + 1]).then_inc(ex_ready, 1)
                                dve.wait_ge(exped, k + 1)
                                v.tensor_tensor(G[s][:, :, 0:D], G[s][:, :, 0:D], ex[s][:, 1, :].unsqueeze(2).to_broadcast([P, L, D]), ALU.mult).then_inc(ex_ready, 1)
                                dve.wait_ge(ex_ready, 2 * k + 2)
                                v.tensor_tensor_scan(S[s][:, :, D], ex[s][:, 0, :], ex[s][:, 1, :], S[1 - s][:, L - 1, D:D + 1], ALU.mult, ALU.add)
                            keep = ex[s][:, 0, :] if kind == "att" else same[s][:]
                            for f in range(D):
                                last = v.tensor_tensor_scan(S[s][:, :, f], keep, G[s][:, :, f], S[1 - s][:, L - 1, f:f + 1], ALU.mult, ALU.add)
                            last.then_inc(scanned, 1)
                    if counts:
                        dve.wait_ge(counted, 1)
                        v.tensor_copy(count[:], C[:, 0:HT])
                    if c1 < NCH:
                        dve.wait_ge(scanned, NC + PRIMED)
                        v.tensor_copy(wsum_state[:], S[1][:, L - 1, :])

                @block.scalar
                def _(act):
                    for s in range(2):
                        act.sem_inc(stored[s], 16)
                    if pooled:
                        act.sem_inc(pstored, 16)
                    with act.Fori(0, NC // 2) as i:
                        for s in range(2):
                            if pooled:
                                act.wait_ge(pscanned, 2 * i + s + 2)
                                act.dma_start(scan_pool[0:EP, :].rearrange("(p j) f -> p j f", p=P)[:, bass.ds((2 * i + s) * SIDE, SIDE), :],
                                              pS[:]).then_inc(pstored, 16)
                            if kind == "att":
                                act.wait_ge(ex_ready, 4 * i + 2 * s + 1)
                                nc.scalar.activation(ex[s][:], ex[s][:], ACT.Exp).then_inc(exped, 1)
                            act.wait_ge(scanned, 2 * i + s + 1 + PRIMED)
                            act.dma_start(rows_out[0:EP, :].rearrange("(p j) f -> p j f", p=P)[:, bass.ds((2 * i + (s + c0)) * L, L), :],
                                          S[s][:]).then_inc(stored[s], 16)
                    for s in range(2):
                        act.wait_ge(stored[s], 16 + 16 * (NC // 2))
                    if pooled:
                        act.wait_ge(pstored, 16 + 16 * NC)

                if counts:
                    @block.tensor
                    def _(pe):
                        mm = nc.tensor.matmul
                        pe.wait_ge(zeroed, 1)
                        mm(C[:, 0:HT], zero_b[:], zero_b[:, 0:HT], start=True, stop=False, skip_group_check=True)
                        for b in range(2):
                            pe.sem_inc(oh_used, 1)
                        with pe.Fori(0, NC // 2) as i:
                            for g in range(2 * HG):
                                pe.wait_ge(oh_ready, 2 * HG * i + g + 1)
                                for j in range(HL):
                                    last = mm(C[:, 0:HT], low[g % 2][:, j, :], high[g % 2][:, j, :],
                                              start=False, stop=False, skip_group_check=True)
                                last.then_inc(oh_used, 1)
                        mm(C[:, 0:HT], zero_b[:], zero_b[:, 0:HT], start=False, stop=True, skip_group_check=True).then_inc(counted, 1)

        def places(by, count, first, end, base):
            with ExitStack() as c:
                ones = sb(f"ones_{by}", [P, P], c=c)
                flag = sb(f"flag_{by}", [P, HT], c=c)
                tile_end = sb(f"tile_end_{by}", [P, HT], c=c)
                last_place = sb(f"last_place_{by}", [P, HT], c=c)
                within, total = ps(f"within_{by}", [P, 512], c=c), ps(f"total_{by}", [P, 512], c=c)
                s_ones, s_sum, s_steps = (semaphore(f"{n}_{by}", c) for n in ("ones_made", "prefix_ready", "place_steps"))
                block = phase(c)

                @block.vector
                def _(dve):
                    v = nc.vector
                    steps = Steps(dve, s_steps)
                    v.memset(ones[:], 1.0).then_inc(s_ones, 1)
                    dve.wait_ge(s_ones, 1)
                    dve.wait_ge(s_sum, 1)
                    steps.done(v.tensor_tensor_scan(tile_end[:], ones[:, 0:HT], total[:, 0:HT], 0.0, ALU.mult, ALU.add))
                    steps.done(v.tensor_tensor(tile_end[:], tile_end[:], total[:, 0:HT], ALU.subtract))
                    steps.done(v.tensor_tensor(first[:], tile_end[:], within[:, 0:HT], ALU.add))
                    steps.done(v.tensor_scalar(flag[:], count[:], 0.0, None, ALU.is_gt))
                    steps.done(v.tensor_tensor(last_place[:], first[:], count[:], ALU.add))
                    steps.done(v.tensor_scalar(last_place[:], last_place[:], -1.0 - EP, None, ALU.add))
                    steps.done(v.tensor_tensor(last_place[:], last_place[:], flag[:], ALU.mult))
                    steps.done(v.tensor_scalar(last_place[:], last_place[:], float(EP), None, ALU.add))
                    steps.done(v.tensor_copy(end[:], last_place[:]))
                    if base:
                        steps.done(v.tensor_scalar(first[:], first[:], float(base), None, ALU.add))

                @block.tensor
                def _(pe):
                    pe.wait_ge(s_ones, 1)
                    nc.tensor.matmul(within[:, 0:HT], below_b[:], count[:], start=True, stop=True)
                    nc.tensor.matmul(total[:, 0:HT], ones[:], count[:], start=True, stop=True).then_inc(s_sum, 1)

        def scatter_by_source(ahead):
            AHEAD = 4
            with ExitStack() as c:
                def slots(name, shape, dt=F32, n=2):
                    return [sb(f"sort_{name}{s}", shape, dt, c) for s in range(n)]

                def sem(name):
                    return semaphore(f"sort_{name}", c)

                feat = slots("feat", [P, L, A])
                row = slots("row", [P, L, A + 1])
                keys = slots("keys", [P, L], I32)
                place = slots("place", [P, L])
                place_i = slots("place_i", [P, L], I32)
                parts_i = sb("sort_parts_i", [P, 2, L], I32, c)
                parts = sb("sort_parts", [P, 2, L], F32, c)
                low = slots("low", [P, P], BF16, 4)
                high = slots("high", [P, HT], BF16, 6)
                lowT = slots("lowT", [P, P], BF16, 4)
                lowTf = slots("lowTf", [P, P], F32, 4)
                before = slots("before", [P, P], BF16, 4)
                counts = slots("counts", [P, HT])
                junk = slots("junk", [P, HT])
                ident_b = sb("ident_b", [P, P], BF16, c)
                pT = [ps(f"pT{s}", [P, 1024], BF16, c) for s in range(2)]
                pS = [ps(f"pS{s}", [P, 512], F32, c) for s in range(2)]
                pG = [ps(f"pG{s}", [P, 512], F32, c) for s in range(3)]
                pC = ps("pC", [P, 512], F32, c)
                loaded = [sem(f"loaded{s}") for s in range(2)]
                scattered = [semaphore(f"scattered{s}") for s in range(2)]
                (rows_ready, rows_used, split, parted, onehot, turned, turned_copied, same_low, before_ready, summed,
                 counted, copied, placed, place_ready, cleared, issuing) = (
                    sem(n) for n in ("rows_ready", "rows_used", "split", "parted", "onehot", "turned", "turned_copied",
                                     "same_low", "before_ready", "summed", "counted", "copied", "placed", "place_ready",
                                     "cleared", "issuing"))
                primed, index_loaded = sem("primed"), sem("index_loaded")
                block = phase(c)
                PIECES = 10 if L % 20 == 0 else L // 2
                PIECE, EVERY = L // PIECES, L // 2 // PIECES
                END = NCH * L

                @block.sync
                def _(sp):
                    sp.dma_start(ahead["index"][:], src[:, NCH // 3 * L:(NCH // 3 + 1) * L]).then_inc(index_loaded, 16)
                    with sp.Fori(0, NCH // 2) as i:
                        for s in range(2):
                            at = (2 * i + s) * L
                            sp.wait_ge(rows_ready, 2 * i + s + 1)
                            sp.wait_ge(parted, 2 * i + s + 1)
                            sp.dma_start(keys[s][:], src[:, bass.ds(at, L)]).then_inc(loaded[s], 16)
                            sp.dma_start(feat[s][:], attr.rearrange("(p j) f -> p j f", p=P)[:, bass.ds(at, L), :]).then_inc(loaded[s], 16)

                @block.gpsimd
                def _(pool):
                    def issue(k, s, n):
                        pool.wait_ge(rows_ready, k + 3)
                        pool.wait_ge(place_ready, k + 2)
                        pool.sem_inc(issuing, 1)
                        for j in range(L):
                            pool.indirect_dma_start(
                                out=by_src, out_offset=bass.IndirectOffsetOnAxis(ap=place_i[s][:, j:j + 1], axis=0),
                                in_=row[s][:, j, :], in_offset=None).then_inc(scattered[s], 16)
                            if j == L // 4 and n is not None:
                                pool.wait_ge(scattered[1 - s], 16 * L * n)
                                pool.sem_inc(rows_used, 1)

                    for n in range(3):
                        pool.sem_inc(rows_used, 1)
                    pool.wait_ge(index_loaded, 16)
                    for j in range(L):
                        pool.indirect_dma_start(
                            out=ahead["rows"][:, j, :], out_offset=None, in_=h_table,
                            in_offset=bass.IndirectOffsetOnAxis(ap=ahead["index"][:, j:j + 1], axis=0)
                        ).then_inc(ahead["gathered"], 16)
                    issue(0, 0, None)
                    with pool.Fori(0, NCH // 2 - 1) as i:
                        issue(2 * i + 1, 1, i + 1)
                        issue(2 * i + 2, 0, i + 1)
                    issue(NCH - 1, 1, NCH // 2)
                    pool.wait_ge(scattered[0], 16 * L * (NCH // 2))
                    pool.wait_ge(scattered[1], 16 * L * (NCH // 2))

                @block.vector
                def _(dve):
                    v = nc.vector

                    def mask(t, q):
                        dve.wait_ge(same_low, t + AHEAD)
                        v.tensor_tensor(before[q % 4][:], pS[q % 2][:, 0:P], below_b[:], ALU.mult).then_inc(before_ready, 1)

                    def pick(t, q, s):
                        dve.wait_ge(summed, t + AHEAD)
                        dve.wait_ge(placed, t - 1 + AHEAD)
                        v.tensor_tensor_reduce(out=junk[q % 2][:], in0=pG[q % 3][:, 0:HT], in1=high[q % 6][:], scale=1.0, scalar=0.0,
                                               op0=ALU.mult, op1=ALU.add, accum_out=place[s][:, q:q + 1]).then_inc(placed, 1)

                    def hand_on(k, t, s):
                        dve.wait_ge(placed, t + 1 + AHEAD)
                        dve.wait_ge(rows_used, k + 2)
                        v.tensor_copy(place_i[s][:], place[s][:]).then_inc(place_ready, 1)

                    for tile in (*low, *high, *lowT, *lowTf, *before, *place):
                        v.memset(tile[:], 0.0)
                    for b in range(2):
                        v.tensor_copy(counts[b][:], first_src[:])
                    v.tensor_copy(ident_b[:], ident[:]).then_inc(cleared, 1)
                    dve.wait_ge(cleared, 1)
                    for n in range(AHEAD):
                        dve.sem_inc(before_ready, 1)
                        dve.sem_inc(placed, 1)
                    for n in range(2):
                        dve.sem_inc(parted, 1)
                    with dve.Fori(0, NCH // 2) as i:
                        for s in range(2):
                            k = 2 * i + s
                            dve.wait_ge(loaded[s], 32 * i + 32)
                            v.tensor_scalar(parts_i[:, 0, :], keys[s][:], 127, None, ALU.bitwise_and)
                            v.tensor_scalar(parts_i[:, 1, :], keys[s][:], 7, None, ALU.logical_shift_right).then_inc(split, 1)
                            dve.wait_ge(split, k + 1)
                            v.tensor_copy(parts[:], parts_i[:]).then_inc(parted, 1)
                            dve.wait_ge(parted, k + 3)
                            for q in range(L):
                                t = k * L + q
                                dve.wait_ge(placed, t - 1 + AHEAD)
                                dve.wait_ge(counted, t - 1 + AHEAD)
                                v.tensor_scalar(low[q % 4][:], iota_b[:], parts[:, 0, q:q + 1], None, ALU.is_equal)
                                v.tensor_scalar(high[q % 6][:], iota_b[:, 0:HT], parts[:, 1, q:q + 1], None, ALU.is_equal).then_inc(onehot, 1)
                                mask(t, (q - 2) % L)
                                pick(t, (q - 4) % L, s if q >= 4 else 1 - s)
                                if q == 3:
                                    hand_on(k - 1, t, 1 - s)
                    for n in range(4):
                        if n < 2:
                            mask(END + n, L - 2 + n)
                        pick(END + n, L - 4 + n, 1)
                    hand_on(NCH - 1, END + 3, 1)

                @block.scalar
                def _(act):
                    a = nc.scalar
                    act.wait_ge(cleared, 1)
                    for n in range(AHEAD):
                        act.sem_inc(turned_copied, 1)
                        act.sem_inc(copied, 1)
                    for n in range(2):
                        act.sem_inc(rows_ready, 1)

                    def keep_counts(t, q):
                        act.wait_ge(counted, t + 1 + AHEAD)
                        a.copy(counts[(q + 1) % 2][:], pC[:, 0:HT]).then_inc(copied, 1)

                    with act.Fori(0, NCH // 2) as i:
                        for s in range(2):
                            k = 2 * i + s
                            act.wait_ge(loaded[s], 32 * i + 32)
                            for q in range(L):
                                t = k * L + q
                                act.wait_ge(turned, t + 1)
                                a.copy(lowT[q % 4][:], pT[q % 2][:, 0:P])
                                a.copy(lowTf[q % 4][:], pT[q % 2][:, 0:P]).then_inc(turned_copied, 1)
                                keep_counts(t, (q - 2) % L)
                                if q == L // 2:
                                    act.wait_ge(rows_used, k + 2)
                                    a.copy(row[s][:, :, A], keys[s][:])
                                if q >= L // 2 and (q - L // 2) % EVERY == 0:
                                    e = (q - L // 2) // EVERY * PIECE
                                    last = a.copy(row[s][:, e:e + PIECE, 0:A], feat[s][:, e:e + PIECE, :])
                                    if e + PIECE == L:
                                        last.then_inc(rows_ready, 1)
                    keep_counts(END, L - 2)

                @block.tensor
                def _(pe):
                    mm = nc.tensor.matmul
                    pe.wait_ge(cleared, 1)
                    mm(pC[:, 0:HT], ident[:], first_src[:], start=True, stop=False, skip_group_check=True)
                    for b in range(2):
                        mm(pS[b][:, 0:P], low[0][:], low[0][:], start=True, stop=True)
                    for b in range(3):
                        last = mm(pG[b][:, 0:HT], low[0][:], high[0][:], start=True, stop=True, skip_group_check=True)
                    last.then_inc(primed, 1)
                    pe.wait_ge(primed, 1)
                    for n in range(AHEAD):
                        pe.sem_inc(same_low, 1)
                        pe.sem_inc(summed, 1)
                        pe.sem_inc(counted, 1)

                    def count(t, q):
                        pe.wait_ge(copied, t + AHEAD)
                        mm(pC[:, 0:HT], low[q % 4][:], high[q % 6][:], start=False, stop=False,
                           skip_group_check=True).then_inc(counted, 1)
                        pe.wait_ge(placed, t + AHEAD)
                        mm(pG[q % 3][:, 0:HT], lowTf[q % 4][:], counts[q % 2][:], start=True, stop=False, skip_group_check=True)

                    def add_before(t, q):
                        pe.wait_ge(before_ready, t + AHEAD)
                        mm(pG[q % 3][:, 0:HT], before[q % 4][:], high[q % 6][:], start=False, stop=True,
                           skip_group_check=True).then_inc(summed, 1)

                    def pairs(t, q):
                        pe.wait_ge(turned_copied, t + AHEAD)
                        mm(pS[q % 2][:, 0:P], lowT[q % 4][:], lowT[q % 4][:], start=True, stop=True).then_inc(same_low, 1)

                    with pe.Fori(0, NCH // 2) as i:
                        for s in range(2):
                            for q in range(L):
                                t = (2 * i + s) * L + q
                                pe.wait_ge(onehot, t + 1)
                                nc.tensor.transpose(pT[q % 2][:, 0:P], low[q % 4][:], ident_b[:]).then_inc(turned, 1)
                                count(t, (q - 2) % L)
                                add_before(t, (q - 3) % L)
                                pairs(t, (q - 1) % L)
                    count(END, L - 2)
                    add_before(END, L - 3)
                    pairs(END, L - 1)
                    count(END + 1, L - 1)
                    add_before(END + 1, L - 2)
                    add_before(END + 2, L - 1)

        fetched = [[semaphore(f"fetched{way}_{n}") for n in range(NPC)] for way in range(2)]

        def fetch(pool, rows, end, V, way):
            for h in range(HT):
                pool.indirect_dma_start(out=V[:, h, :], out_offset=None, in_=rows,
                                        in_offset=bass.IndirectOffsetOnAxis(ap=end[:, h:h + 1], axis=0)).then_inc(fetched[way][h // TP], 16)

        def await_group(engine, g, way, nth):
            engine.wait_ge(fetched[way][g * TG // TP], 16 * TP * nth)

        def await_fetch(engine, way, nth):
            for piece in fetched[way]:
                engine.wait_ge(piece, 16 * TP * nth)

        class Carry:

            def __init__(self, kind, rows, F, c, pR):
                self.kind, self.rows, self.F, self.pR = kind, rows, F, pR
                key_t = F32 if kind == "pool" else I32
                self.edge_keys = sb(f"{kind}_edge_keys", [P, 4], key_t, c)
                self.ek = sb(f"{kind}_ek", [P, 4], F32, c)
                self.fl = sb(f"{kind}_fl", [P, 8], F32, c)
                self.tail = sb(f"{kind}_tail", [P, F], F32, c)
                self.tailT, self.contT, self.fullT, self.tmT = (sb(f"{kind}_{n}T", [F, P], F32, c) for n in ("tail", "cont", "full", "tm"))
                self.d0, self.d1, self.cinT, self.mc, self.tmp = (sb(f"{kind}_{n}", [F, P], F32, c) for n in ("d0", "d1", "cinT", "mc", "tmp"))
                self.cin = sb(f"{kind}_cin", [P, F + 1], F32, c)
                self.fk = sb(f"{kind}_fk", [P, NG], F32, c)
                self.s_keys, self.s_tail, self.s_flags, self.s_T, self.s_cinT, self.s_cinP, self.s_cin, self.s_e, self.s_exp = (
                    semaphore(f"{kind}_c_{n}", c) for n in
                    ("keys", "tail", "flags", "turned", "cinT", "cin_turned", "cin", "expo", "exped"))

            def load(self, sp):
                if self.kind == "pool":
                    col = lambda off, at: by_src[off:EP + off, A:A + 1].rearrange("(p j) o -> p (j o)", p=P)[:, at:at + 1]
                else:
                    col = lambda off, at: dst[off:EP + off].rearrange("(p j) -> p j", p=P)[:, at:at + 1]
                for n, (off, at) in enumerate(((1, 0), (0, 0), (1, J - 1), (2, J - 1))):
                    sp.dma_start(self.edge_keys[:, n:n + 1], col(off, at), allow_slow_non_contiguous=True).then_inc(self.s_keys, 16)
                sp.dma_start(self.tail[:], self.rows[0:EP, :].rearrange("(p j) f -> p j f", p=P)[:, J - 1, :]).then_inc(self.s_tail, 16)

            def vector(self, dve, st):
                v, F, kind, pR = nc.vector, self.F, self.kind, self.pR
                ek, fl, fk, d0, d1, cinT, mc, tmp, cin, contT, tmT = (
                    self.ek, self.fl, self.fk, self.d0, self.d1, self.cinT, self.mc, self.tmp, self.cin, self.contT, self.tmT)
                dve.wait_ge(self.s_keys, 64)
                st.done(v.tensor_copy(ek[:], self.edge_keys[:]))
                cont, full, contn, valid = (fl[:, n:n + 1] for n in range(4))
                v.tensor_tensor(cont, ek[:, 0:1], ek[:, 1:2], ALU.is_equal)
                v.tensor_tensor(full, ek[:, 0:1], ek[:, 2:3], ALU.is_equal)
                st.done(v.tensor_tensor(contn, ek[:, 2:3], ek[:, 3:4], ALU.is_equal))
                st.done(v.tensor_tensor(valid, full, contn, ALU.mult))
                st.done(v.tensor_scalar(valid, valid, -1.0, 1.0, ALU.mult, ALU.add))
                st.done(v.tensor_tensor(valid, valid, cont, ALU.mult))
                st.done(v.tensor_scalar(fl[:, 4:5], ek[:, 0:1], 1.0, None, ALU.add))
                st.done(v.tensor_tensor(fl[:, 4:5], fl[:, 4:5], valid, ALU.mult))
                for g in range(NG):
                    last = v.tensor_scalar(fk[:, g:g + 1], fl[:, 4:5], -1.0 - g * TG * P, None, ALU.add)
                last.then_inc(self.s_flags, 1)
                dve.wait_ge(self.s_flags, 1)
                dve.wait_ge(self.s_T, 1)
                v.tensor_copy(self.tailT[:], pR[0][0:F, 0:P])
                v.tensor_copy(contT[:], pR[1][0:F, 0:P])
                if kind == "att":
                    v.tensor_copy(tmT[:], pR[1][0:F, 2 * P:3 * P])
                st.done(v.tensor_copy(self.fullT[:], pR[1][0:F, P:2 * P]))
                c1, f1, t1 = contT[:, 1:P], self.fullT[:, 0:P - 1], self.tailT[:, 0:P - 1]
                v.memset(d0[:, 0:1], 0.0)
                v.memset(d1[:, 0:1], 0.0)
                st.done(v.tensor_tensor(d0[:, 1:P], c1, f1, ALU.mult))
                if kind == "att":
                    m1 = tmT[:, 0:P - 1]
                    v.memset(cinT[:, 0:1], LOW)
                    v.memset(tmp[:, 0:1], LOW)
                    st.done(v.tensor_scalar(cinT[:, 1:P], c1, -LOW, LOW, ALU.mult, ALU.add))
                    st.done(v.tensor_scalar(tmp[:, 1:P], d0[:, 1:P], -LOW, LOW, ALU.mult, ALU.add))
                    st.done(v.tensor_tensor(d1[:, 1:P], m1, c1, ALU.mult))
                    st.done(v.tensor_tensor(cinT[:, 1:P], cinT[:, 1:P], d1[:, 1:P], ALU.add))
                    st.done(v.tensor_tensor_scan(mc[:], tmp[:], cinT[:], LOW, ALU.add, ALU.max))
                    v.memset(tmp[:, 0:1], 0.0)
                    st.done(v.tensor_tensor(tmp[:, 1:P], mc[:, 0:P - 1], mc[:, 1:P], ALU.subtract))
                    st.done(v.tensor_scalar(tmp[:], tmp[:], 0.0, None, ALU.min))
                    v.tensor_tensor(d1[:, 1:P], m1, mc[:, 1:P], ALU.subtract).then_inc(self.s_e, 1)
                    dve.wait_ge(self.s_e, 1)
                    v.tensor_scalar(d1[:], d1[:], 0.0, None, ALU.min).then_inc(self.s_e, 1)
                    dve.wait_ge(self.s_exp, 1)
                    st.done(v.tensor_tensor(d0[:], d0[:], tmp[:], ALU.mult))
                    st.done(v.tensor_tensor(d1[:, 1:P], d1[:, 1:P], c1, ALU.mult))
                    st.done(v.tensor_tensor(d1[:, 1:P], d1[:, 1:P], t1, ALU.mult))
                    st.done(v.memset(d1[:, 0:1], 0.0))
                else:
                    st.done(v.tensor_tensor(d1[:, 1:P], t1, c1, ALU.mult))
                if kind == "pool":
                    st.done(v.tensor_tensor_scan(cinT[0:A, :], d0[0:A, :], d1[0:A, :], 0.0, ALU.mult, ALU.add))
                    v.memset(mc[A:F, 0:1], LOW)
                    v.memset(tmp[A:F, 0:1], LOW)
                    st.done(v.tensor_scalar(mc[A:F, 1:P], contT[A:F, 1:P], -LOW, LOW, ALU.mult, ALU.add))
                    st.done(v.tensor_tensor(mc[A:F, 1:P], mc[A:F, 1:P], d1[A:F, 1:P], ALU.add))
                    st.done(v.tensor_scalar(tmp[A:F, 1:P], d0[A:F, 1:P], -LOW, LOW, ALU.mult, ALU.add))
                    v.tensor_tensor_scan(cinT[A:F, :], tmp[A:F, :], mc[A:F, :], LOW, ALU.add, ALU.max).then_inc(self.s_cinT, 1)
                else:
                    v.tensor_tensor_scan(cinT[:], d0[:], d1[:], 0.0, ALU.mult, ALU.add).then_inc(self.s_cinT, 1)
                dve.wait_ge(self.s_cinP, 1)
                if kind == "att":
                    v.tensor_copy(cin[:, F - 1:F], pR[1][:, 0:1])
                    v.tensor_copy(cin[:, 0:F - 1], pR[0][:, 0:F - 1])
                else:
                    v.tensor_copy(cin[:, 0:F], pR[0][:, 0:F])
                v.memset(cin[:, F:F + 1], 1.0).then_inc(self.s_cin, 1)

            def scalar(self, act):
                act.wait_ge(self.s_e, 2)
                nc.scalar.activation(self.tmp[:], self.tmp[:], ACT.Exp)
                nc.scalar.activation(self.d1[:, 1:P], self.d1[:, 1:P], ACT.Exp).then_inc(self.s_exp, 1)

            def tensor(self, pe):
                mm, F, pR, fl, tail = nc.tensor.matmul, self.F, self.pR, self.fl, self.tail
                pe.wait_ge(self.s_tail, 16)
                pe.wait_ge(self.s_flags, 1)
                mm(pR[0][0:F, 0:P], tail[:], ident[:], start=True, stop=True)
                if self.kind == "att":
                    mm(pR[1][0:F, 2 * P:3 * P], tail[:, F - 1:F].to_broadcast([P, F]), ident[:], start=True, stop=True)
                mm(pR[1][0:F, P:2 * P], fl[:, 1:2].to_broadcast([P, F]), ident[:], start=True, stop=True)
                mm(pR[1][0:F, 0:P], fl[:, 0:1].to_broadcast([P, F]), ident[:], start=True, stop=True).then_inc(self.s_T, 1)
                pe.wait_ge(self.s_cinT, 1)
                if self.kind == "att":
                    mm(pR[1][:, 0:F], self.mc[:], ident[0:F, 0:F], start=True, stop=True)
                mm(pR[0][:, 0:F], self.cinT[:], ident[0:F, 0:F], start=True, stop=True).then_inc(self.s_cinP, 1)
                pe.wait_ge(self.s_cin, 1)

            def select(self, g, sel, iota_g):
                return nc.vector.tensor_scalar(sel[g % 2][:], iota_g[:], self.fk[:, g:g + 1], None, ALU.is_equal)

            def hand(self, g, sel, pK):
                for t in range(TG):
                    last = nc.tensor.matmul(pK[:, t * (self.F + 1):(t + 1) * (self.F + 1)], sel[g % 2][:, t * P:(t + 1) * P],
                                            self.cin[:], start=True, stop=True)
                return last

            def view(self, pK):
                return pK[:, 0:TG * (self.F + 1)].rearrange("p (t f) -> p t f", t=TG)

        def first_layers():
            with ExitStack() as c:
                V, VP = sb("V_wsum", [P, HT, D], c=c), sb("V_pool", [P, HT, D], c=c)
                w0, w0T = sb("w0", [D, D], c=c), sb("w0T", [D, D], c=c)
                w1, w2 = sb("w1", [3 * A + 1, HID], c=c), sb("w2", [HID, D], c=c)
                wr = sb("wr", [D, R, D], c=c)
                bias0, bias2 = sb("bias0", [P, D], c=c), sb("bias2", [P, D], c=c)
                b_hid, u_b = sb("b_hid", [P, 1], c=c), sb("u_b", [P, 1], c=c)
                iota_g = sb("iota_g1", [P, TG * P], c=c)
                sel = [sb(f"sel1_{s}", [P, TG * P], c=c) for s in range(2)]
                rcount = sb("rcount", [P, HT], c=c)
                absent = sb("absent", [P, TG], c=c)
                carried_max = sb("carried_max", [P, TG, A], c=c)
                V3 = [sb(f"V3_{s}", [P, TG, 3 * A + 1], c=c) for s in range(2)]
                square = sb("square1", [P, TG, D], c=c)
                VT = sb("VT", [3 * A + 1, TG * P], c=c)
                hid = sb("hid", [P, TG * P], c=c)
                HTt = [sb(f"HTt{s}", [D, TG * P], c=c) for s in range(2)]
                made = [sb(f"made{s}", [P, TG, R * D], c=c) for s in range(2)]
                pK = ps("pK1", [P, 512], c=c)
                pV = ps("pV1", [P, 1024], c=c)
                pH = ps("pH1", [P, 1024], c=c)
                pO = ps("pO1", [P, 512], c=c)
                pW = [ps(f"pW1_{s}", [P, 512], c=c) for s in range(2)]
                (s_w, s_iota, s_wt, s_wT, s_steps, s_sel, s_K, s_rows, s_turned, s_VT, s_hidP, s_hid, s_out, s_added,
                 s_var, s_root, s_h, s_hturned, s_HT, s_prod, s_made) = (
                    semaphore(f"fl_{n}", c) for n in
                    ("weights", "iota", "w_turned", "wT", "steps", "sel", "K", "rows", "turned", "VT", "hidP", "hid", "out",
                     "added", "var", "root", "h", "h_turned", "HT", "prod", "made"))
                s_stored = [semaphore(f"fl_stored{s}", c) for s in range(2)]
                pR = [pH[:, 0:512], pH[:, 512:1024]]
                wsum, pooled = Carry("wsum", scan_wsum, D, c, pR), Carry("pool", scan_pool, D, c, pR)
                block = phase(c)
                NW = 16 * 8
                out_view = pO[:, 0:TG * D].rearrange("p (t d) -> p t d", t=TG)

                @block.sync
                def _(sp):
                    pooled.load(sp)
                    wsum.load(sp)
                    for tile, a in ((w0, W0), (w1, W1), (w2, W2), (bias0, b0.unsqueeze(0).to_broadcast([P, D])),
                                    (bias2, b2.unsqueeze(0).to_broadcast([P, D])), (wr, Wr.rearrange("r d f -> d r f"))):
                        sp.dma_start(tile[:], a).then_inc(s_w, 16)
                    sp.dma_start(b_hid[:], b1.unsqueeze(1), allow_slow_non_contiguous=True).then_inc(s_w, 16)
                    sp.dma_start(u_b[:], u[0:1, 0:1].to_broadcast([P, 1]), allow_slow_non_contiguous=True).then_inc(s_w, 16)
                    for g in range(NG):
                        sp.wait_ge(s_made, TG * (g + 1))
                        sp.dma_start(rel_table.rearrange("(h p r) d -> p h (r d)", p=P, r=R)[:, g * TG:(g + 1) * TG, :],
                                     made[g % 2][:]).then_inc(s_stored[g % 2], 16)
                    for s in range(2):
                        sp.wait_ge(s_stored[s], 16 * (NG // 2))

                @block.gpsimd
                def _(pool):
                    nc.gpsimd.iota(iota_g[:], [[1, TG * P]], base=0, channel_multiplier=0,
                                   allow_small_or_imprecise_dtypes=True).then_inc(s_iota, 1)
                    fetch(pool, scan_pool, end_src, VP, 1)
                    fetch(pool, scan_wsum, end_dst, V, 0)
                    await_fetch(pool, 1, 1)
                    await_fetch(pool, 0, 1)

                @block.vector
                def _(dve):
                    v = nc.vector
                    st = Steps(dve, s_steps)
                    pooled.vector(dve, st)
                    wsum.vector(dve, st)
                    dve.wait_ge(s_w, NW)
                    dve.wait_ge(s_wt, 1)
                    v.tensor_copy(w0T[:], pO[0:D, 0:D]).then_inc(s_wT, 1)
                    dve.wait_ge(s_iota, 1)
                    for g in range(2):
                        pooled.select(g, sel, iota_g).then_inc(s_sel, 1)
                    st.done(v.tensor_tensor(bias0[:], bias0[:], bias2[:], ALU.add))
                    st.done(v.tensor_tensor(X[:], X[:], bias0[:].unsqueeze(1).to_broadcast([P, HT, D]), ALU.add))
                    st.done(v.tensor_scalar(rcount[:], count_src[:], 1.0, None, ALU.max))
                    st.done(v.reciprocal(rcount[:], rcount[:]))
                    for s in range(2):
                        v.tensor_copy(V3[s][:, :, 3 * A:3 * A + 1], u_b[:].unsqueeze(1).to_broadcast([P, TG, 1]))

                    def add_out(n):
                        dve.wait_ge(s_out, n + 1)
                        xg = tiles(X, n % NG)
                        v.tensor_tensor(xg, xg, out_view, ALU.add).then_inc(s_added, 1)
                        dve.wait_ge(s_added, n + 1)

                    for g in range(NG):
                        K3, v3 = pooled.view(pK), V3[g % 2]
                        await_group(dve, g, 1, 1)
                        dve.wait_ge(s_K, g + 1)
                        if g >= 2:
                            dve.wait_ge(s_turned, g - 1)
                        v.tensor_tensor(v3[:, :, 0:A], tiles(VP, g)[:, :, 0:A], K3[:, :, 0:A], ALU.add)
                        st.done(v.tensor_scalar(absent[:], K3[:, :, D], -LOW, LOW, ALU.mult, ALU.add))
                        v.tensor_tensor(v3[:, :, 2 * A:3 * A], v3[:, :, 0:A], group_wide(rcount, g, A), ALU.mult)
                        st.done(v.tensor_tensor(carried_max[:], K3[:, :, A:D], absent[:].unsqueeze(2).to_broadcast([P, TG, A]), ALU.add))
                        v.tensor_tensor(v3[:, :, A:2 * A], tiles(VP, g)[:, :, A:D], carried_max[:], ALU.max).then_inc(s_rows, 1)
                        n = g + 2
                        (pooled if n < NG else wsum).select(n % NG, sel, iota_g).then_inc(s_sel, 1)
                        if g >= 1:
                            add_out(g - 1)
                    add_out(NG - 1)
                    norm = GroupNorm(dve, st, square, s_var, s_root)
                    for n in range(NG + 2):
                        if n >= 2:
                            norm.scale(n - 2, tiles(H, n - 2)).then_inc(s_h, 1)
                        if n < NG:
                            await_group(dve, n, 0, 1)
                            dve.wait_ge(s_K, NG + n + 1)
                            v.tensor_tensor(tiles(V, n), tiles(V, n), wsum.view(pK)[:, :, 0:D], ALU.add).then_inc(s_rows, 1)
                            if n + 2 < NG:
                                wsum.select(n + 2, sel, iota_g).then_inc(s_sel, 1)
                        if 1 <= n <= NG:
                            add_out(NG + n - 1)
                            norm.centre(n - 1)

                @block.scalar
                def _(act):
                    a = nc.scalar

                    def copy_turned(n, F):
                        act.wait_ge(s_turned, n + 1)
                        a.copy(VT[0:F, :], pV[0:F, 0:TG * P]).then_inc(s_VT, 1)

                    for g in range(NG):
                        copy_turned(g, 3 * A + 1)
                        act.wait_ge(s_hidP, g + 1)
                        a.activation(hid[:], pH[:, 0:TG * P], ACT.Relu, bias=b_hid[:, 0:1]).then_inc(s_hid, 1)
                    for n in range(1, NG + 2):
                        if n >= 2:
                            act.wait_ge(s_hturned, n - 1)
                            if n >= 4:
                                act.wait_ge(s_prod, TG * (n - 3))
                            a.copy(HTt[n % 2][:], pV[0:D, 0:TG * P]).then_inc(s_HT, 1)
                        if n <= NG:
                            copy_turned(NG + n - 1, D)
                        if n >= 2:
                            for t in range(TG):
                                if t == 0 and n >= 4:
                                    act.wait_ge(s_stored[n % 2], 16 * (n // 2 - 1))
                                k = TG * (n - 2) + t
                                act.wait_ge(s_prod, k + 1)
                                a.copy(made[n % 2][:, t, :], pW[k % 2][:]).then_inc(s_made, 1)
                                if t == 4 and n <= NG:
                                    group_root(act, n - 1, s_var, s_root)
                        else:
                            group_root(act, n - 1, s_var, s_root)

                @block.tensor
                def _(pe):
                    mm = nc.tensor.matmul
                    pooled.tensor(pe)
                    wsum.tensor(pe)
                    pe.wait_ge(s_w, NW)
                    nc.tensor.transpose(pO[0:D, 0:D], w0[:], ident[0:D, 0:D]).then_inc(s_wt, 1)
                    pe.wait_ge(s_wT, 1)

                    def hand(n):
                        pe.wait_ge(s_sel, n + 1)
                        (pooled if n < NG else wsum).hand(n % NG, sel, pK).then_inc(s_K, 1)

                    def turn(rows, F):
                        for t in range(TG):
                            last = nc.tensor.transpose(pV[0:F, t * P:(t + 1) * P], rows[:, t, 0:F], ident[:])
                        return last

                    def project(n, left, w):
                        if n > 0:
                            pe.wait_ge(s_added, n)
                        for t in range(TG):
                            last = mm(pO[:, t * D:(t + 1) * D], left[:, t * P:(t + 1) * P], w[:], start=True, stop=True)
                        last.then_inc(s_out, 1)

                    def relations(n, t0, t1):
                        for t in range(t0, t1):
                            k = TG * n + t
                            if k >= 2:
                                pe.wait_ge(s_made, k - 1)
                            mm(pW[k % 2][:], HTt[n % 2][:, t * P:(t + 1) * P], wr[:].rearrange("d r f -> d (r f)"),
                               start=True, stop=True).then_inc(s_prod, 1)

                    hand(0)
                    for g in range(NG + 1):
                        if g < NG:
                            pe.wait_ge(s_rows, g + 1)
                            turn(V3[g % 2], 3 * A + 1).then_inc(s_turned, 1)
                            hand(g + 1)
                        if g >= 1:
                            pe.wait_ge(s_hid, g)
                            project(g - 1, hid, w2)
                        if g < NG:
                            pe.wait_ge(s_VT, g + 1)
                            mm(pH[:, 0:512], w1[:], VT[:, 0:512], start=True, stop=True)
                            mm(pH[:, 512:TG * P], w1[:], VT[:, 512:TG * P], start=True, stop=True).then_inc(s_hidP, 1)
                    for n in range(1, NG + 2):
                        if n >= 2:
                            pe.wait_ge(s_h, n - 1)
                            turn(tiles(H, n - 2), D).then_inc(s_hturned, 1)
                        if n <= NG:
                            pe.wait_ge(s_rows, NG + n)
                            if n < NG:
                                hand(NG + n)
                            if n >= 2:
                                pe.wait_ge(s_HT, n - 1)
                            turn(tiles(V, n - 1), D).then_inc(s_turned, 1)
                        if n >= 2:
                            pe.wait_ge(s_HT, n - 1)
                            relations(n - 2, 0, 2)
                        if n <= NG:
                            pe.wait_ge(s_VT, NG + n)
                            project(NG + n - 1, VT[0:D, :], w0T)
                        if n >= 2:
                            relations(n - 2, 2, TG)

        def relation_update():
            with ExitStack() as c:
                V = sb("V_rel", [P, HT, D], c=c)
                al, ar = (sb(n, [P, D], F32, c) for n in ("al", "ar"))
                zt = sb("zt", [P, HT, D + 1], F32, c)
                er = sb("er_nodes", [P, HT], F32, c)
                at_f, node, keep_h, by_degree = (sb(n, [P, HT], F32, c) for n in ("at_f", "node", "keep_h", "by_degree"))
                at_i = sb("at_i", [P, HT], I32, c)
                iota_g = sb("iota_g2", [P, TG * P], c=c)
                sel = [sb(f"sel2_{s}", [P, TG * P], c=c) for s in range(2)]
                square, part, dots = (sb(n, [P, TG, D], c=c) for n in ("square2", "part", "dots"))
                pK = [ps(f"pK2_{s}", [P, 512], c=c) for s in range(2)]
                pR = [ps(f"pR2_{s}", [P, 512], c=c) for s in range(2)]
                s_w, s_node, s_steps, s_sel, s_K, s_rows, s_var, s_root, s_table, s_er, s_stored = (
                    semaphore(f"ru_{n}", c) for n in
                    ("weights", "node", "steps", "sel", "K", "rows", "var", "root", "table", "er", "stored"))
                s_spread = semaphore("er_spread")
                carry = Carry("rel", scan_rel, D, c, pR)
                block = phase(c)

                @block.sync
                def _(sp):
                    carry.load(sp)
                    sp.dma_start(al[:], attn_l.unsqueeze(0).to_broadcast([P, D])).then_inc(s_w, 16)
                    sp.dma_start(ar[:], attn_r.unsqueeze(0).to_broadcast([P, D])).then_inc(s_w, 16)
                    for n in range(NPC):
                        sp.wait_ge(s_table, 2 * n + 2)
                        sp.dma_start(att_table.rearrange("(h p) d -> p h d", p=P)[:, n * TP:(n + 1) * TP, :],
                                     zt[:, n * TP:(n + 1) * TP, :]).then_inc(s_stored, 16)
                    sp.dma_start(er_table.rearrange("(h p) o -> p (h o)", p=P), er[:], allow_slow_non_contiguous=True).then_inc(s_stored, 16)
                    sp.wait_ge(s_stored, 16 * NPC + 16)

                @block.gpsimd
                def _(pool):
                    nc.gpsimd.iota(iota_g[:], [[1, TG * P]], base=0, channel_multiplier=0,
                                   allow_small_or_imprecise_dtypes=True).then_inc(s_node, 1)
                    nc.gpsimd.iota(node[:], [[P, HT]], base=EP, channel_multiplier=1,
                                   allow_small_or_imprecise_dtypes=True).then_inc(s_node, 1)
                    fetch(pool, scan_rel, end_dst, V, 0)
                    for h in range(HT):
                        if h % TG == 0:
                            pool.wait_ge(s_er, h // TG + 1)
                        pool.indirect_dma_start(out=er_start, out_offset=bass.IndirectOffsetOnAxis(ap=at_i[:, h:h + 1], axis=0),
                                                in_=er[:, h:h + 1], in_offset=None).then_inc(s_spread, 16)
                    await_fetch(pool, 0, 2)
                    pool.wait_ge(s_spread, 16 * HT)

                @block.vector
                def _(dve):
                    v = nc.vector
                    st = Steps(dve, s_steps)
                    row = lambda a: a[:].unsqueeze(1).to_broadcast([P, TG, D])
                    carry.vector(dve, st)
                    dve.wait_ge(s_node, 2)
                    for g in range(2):
                        carry.select(g, sel, iota_g).then_inc(s_sel, 1)
                    none = stat[:, 3, :]
                    st.done(v.tensor_scalar(none, count_dst[:], 0.0, None, ALU.is_equal))
                    st.done(v.tensor_scalar(at_f[:], count_dst[:], 0.0, None, ALU.is_gt))
                    st.done(v.tensor_tensor(node[:], node[:], none, ALU.mult))
                    st.done(v.tensor_tensor(at_f[:], at_f[:], first_dst[:], ALU.mult))
                    st.done(v.tensor_tensor(at_f[:], at_f[:], node[:], ALU.add))
                    st.done(v.tensor_copy(at_i[:], at_f[:]))
                    st.done(v.tensor_scalar(keep_h[:], none, 0.8, 0.2, ALU.mult, ALU.add))
                    st.done(v.tensor_scalar(by_degree[:], count_dst[:], 1.0, None, ALU.max))
                    st.done(v.reciprocal(by_degree[:], by_degree[:]))
                    st.done(v.tensor_scalar(by_degree[:], by_degree[:], 0.8, None, ALU.mult))
                    dve.wait_ge(s_w, 32)
                    norm = GroupNorm(dve, st, square, s_var, s_root)
                    for g in range(NG + 1):
                        if g < NG:
                            vg, xg = tiles(V, g), tiles(X, g)
                            await_group(dve, g, 0, 2)
                            dve.wait_ge(s_K, g + 1)
                            v.tensor_tensor(vg, vg, carry.view(pK[g % 2])[:, :, 0:D], ALU.add).then_inc(s_rows, 1)
                            if g + 2 < NG:
                                carry.select(g + 2, sel, iota_g).then_inc(s_sel, 1)
                            dve.wait_ge(s_rows, g + 1)
                            v.tensor_tensor(part[:], tiles(H, g), group_wide(keep_h, g, D), ALU.mult)
                            st.done(v.tensor_tensor(vg, vg, group_wide(by_degree, g, D), ALU.mult))
                            st.done(v.tensor_tensor(part[:], part[:], vg, ALU.add))
                            st.done(v.scalar_tensor_tensor(xg, part[:], 0.0, xg, ALU.max, ALU.add))
                            norm.centre(g)
                        if g >= 1:
                            zg = tiles(zt, g - 1)
                            st.done(norm.scale(g - 1, zg[:, :, 0:D]))
                            st.done(v.tensor_tensor(dots[:], zg[:, :, 0:D], row(ar), ALU.mult))
                            v.tensor_reduce(tiles(er, g - 1), dots[:], AX, ALU.add).then_inc(s_er, 1)
                            dve.wait_ge(s_er, g)
                            st.done(v.tensor_tensor(dots[:], zg[:, :, 0:D], row(al), ALU.mult))
                            v.tensor_reduce(zg[:, :, D:D + 1], dots[:], AX, ALU.add).then_inc(s_table, 1)
                            dve.wait_ge(s_table, g)

                @block.scalar
                def _(act):
                    for g in range(NG):
                        group_root(act, g, s_var, s_root)

                @block.tensor
                def _(pe):
                    carry.tensor(pe)
                    for g in range(NG):
                        pe.wait_ge(s_sel, g + 1)
                        if g >= 2:
                            pe.wait_ge(s_rows, g - 1)
                        carry.hand(g, sel, pK[g % 2]).then_inc(s_K, 1)

        def attention_update():
            with ExitStack() as c:
                V = sb("V_att", [P, HT, FM], c=c)
                ea = [sb(f"ea{s}", [P, 2, TG], c=c) for s in range(2)]
                neg = [sb(f"neg{s}", [P, TG, D], c=c) for s in range(2)]
                KW = sb("carried_weighed", [P, TG, D + 1], c=c)
                iota_g = sb("iota_g3", [P, TG * P], c=c)
                sel = [sb(f"sel3_{s}", [P, TG * P], c=c) for s in range(2)]
                pK = [ps(f"pK3_{s}", [P, 512], c=c) for s in range(2)]
                pR = [ps(f"pR3_{s}", [P, 512], c=c) for s in range(2)]
                s_iota, s_steps, s_sel, s_K, s_taken, s_e, s_exp, s_m, s_em, s_x, s_out = (
                    semaphore(f"au_{n}", c) for n in
                    ("iota", "steps", "sel", "K", "taken", "expo", "exped", "neg", "neg_exped", "x", "out"))
                carry = Carry("att", scan_att, FM, c, pR)
                block = phase(c)
                full = N // P

                @block.gpsimd
                def _(pool):
                    nc.gpsimd.iota(iota_g[:], [[1, TG * P]], base=0, channel_multiplier=0,
                                   allow_small_or_imprecise_dtypes=True).then_inc(s_iota, 1)
                    fetch(pool, scan_att, end_dst, V, 1)
                    await_fetch(pool, 1, 2)

                @block.vector
                def _(dve):
                    v = nc.vector
                    st = Steps(dve, s_steps)
                    mi, mx, den = (stat[:, n, :] for n in range(3))
                    carry.vector(dve, st)
                    dve.wait_ge(s_iota, 1)
                    for g in range(2):
                        carry.select(g, sel, iota_g).then_inc(s_sel, 1)
                    for n in range(NG + 2):
                        if n < NG:
                            Kg, b = carry.view(pK[n % 2]), n % 2
                            m_own, mi_g, mx_g = tiles(V, n)[:, :, D + 1], tiles(mi, n), tiles(mx, n)
                            await_group(dve, n, 1, 2)
                            dve.wait_ge(s_K, n + 1)
                            st.done(v.tensor_scalar(mi_g, Kg[:, :, D + 2], -LOW, LOW, ALU.mult, ALU.add))
                            st.done(v.tensor_tensor(mi_g, mi_g, Kg[:, :, D + 1], ALU.add))
                            st.done(v.tensor_tensor(mx_g, mi_g, m_own, ALU.max))
                            v.tensor_tensor(ea[b][:, 0, :], m_own, mx_g, ALU.subtract)
                            v.tensor_tensor(ea[b][:, 1, :], mi_g, mx_g, ALU.subtract).then_inc(s_e, 1)
                            if n + 2 < NG:
                                carry.select(n + 2, sel, iota_g).then_inc(s_sel, 1)
                        if 1 <= n <= NG:
                            g, b = n - 1, (n - 1) % 2
                            vg, hg, xg, dg = tiles(V, g), tiles(H, g), tiles(X, g), tiles(den, g)
                            wide = lambda k: ea[b][:, k, :].unsqueeze(2).to_broadcast([P, TG, D + 1])
                            dve.wait_ge(s_exp, g + 1)
                            v.tensor_tensor(KW[:], carry.view(pK[b])[:, :, 0:D + 1], wide(1), ALU.mult).then_inc(s_taken, 1)
                            dve.wait_ge(s_taken, g + 1)
                            st.done(v.tensor_tensor(vg[:, :, 0:D + 1], vg[:, :, 0:D + 1], wide(0), ALU.mult))
                            st.done(v.tensor_tensor(vg[:, :, 0:D + 1], vg[:, :, 0:D + 1], KW[:], ALU.add))
                            st.done(v.tensor_scalar(dg, vg[:, :, D], 0.5, None, ALU.max))
                            st.done(v.reciprocal(dg, dg))
                            st.done(v.tensor_tensor(hg, vg[:, :, 0:D], dg.unsqueeze(2).to_broadcast([P, TG, D]), ALU.mult))
                            if g >= 2:
                                dve.wait_ge(s_x, g - 1)
                            v.tensor_scalar(neg[b][:], hg, 0.0, None, ALU.min).then_inc(s_m, 1)
                            st.done(v.scalar_tensor_tensor(xg, hg, 0.0, xg, ALU.max, ALU.add))
                        if n >= 2:
                            xg = tiles(X, n - 2)
                            dve.wait_ge(s_em, n - 1)
                            v.scalar_tensor_tensor(xg, neg[n % 2][:], -1.0, xg, ALU.add, ALU.add).then_inc(s_x, 1)

                @block.scalar
                def _(act):
                    carry.scalar(act)
                    for n in range(NG + 1):
                        if n < NG:
                            act.wait_ge(s_e, n + 1)
                            nc.scalar.activation(ea[n % 2][:], ea[n % 2][:], ACT.Exp).then_inc(s_exp, 1)
                        if n >= 1:
                            act.wait_ge(s_m, n)
                            nc.scalar.activation(neg[(n - 1) % 2][:], neg[(n - 1) % 2][:], ACT.Exp).then_inc(s_em, 1)

                @block.tensor
                def _(pe):
                    carry.tensor(pe)
                    for g in range(NG):
                        pe.wait_ge(s_sel, g + 1)
                        if g >= 2:
                            pe.wait_ge(s_taken, g - 1)
                        carry.hand(g, sel, pK[g % 2]).then_inc(s_K, 1)

                @block.sync
                def _(sp):
                    carry.load(sp)
                    stores = 0
                    for t0 in range(0, full, TP):
                        t1 = min(t0 + TP, full)
                        sp.wait_ge(s_x, -(-t1 // TG))
                        sp.dma_start(out[t0 * P:t1 * P, :].rearrange("(h p) d -> p h d", p=P), X[:, t0:t1, :]).then_inc(s_out, 16)
                        stores += 1
                    if N > full * P:
                        sp.wait_ge(s_x, full // TG + 1)
                        sp.dma_start(out[full * P:N, :], X[0:N - full * P, full, :]).then_inc(s_out, 16)
                        stores += 1
                    sp.wait_ge(s_out, 16 * stores)

        gathered_layer("wsum", h_table, D, scan_wsum, 0, NCH // 3, counts=("src", count_src))
        places("src", count_src, first_src, end_src, 1)
        with ExitStack() as c:
            ahead = dict(rows=sb("ahead_rows", [P, L, D], c=c), index=sb("ahead_index", [P, L], I32, c),
                         gathered=semaphore("ahead_gathered"))
            scatter_by_source(ahead)
            gathered_layer("wsum", h_table, D, scan_wsum, NCH // 3, NCH, counts=("dst", count_dst), pooled=True, ahead=ahead)
        places("dst", count_dst, first_dst, end_dst, 0)
        first_layers()
        gathered_layer("rel", rel_table, D, scan_rel, 0, NCH)
        relation_update()
        gathered_layer("att", att_table, D + 1, scan_att, 0, NCH)
        attention_update()


def kernel(x, src, dst, edge_attr_32, edge_type_8, edge_weight1, L0_gnn_W, L0_gnn_b, L1_gnn_u, L1_gnn_W1, L1_gnn_b1,
           L1_gnn_W2, L1_gnn_b2, L2_gnn_weight_r, L3_gnn_attn_l, L3_gnn_attn_r):
    import numpy as np
    import concourse.bacc as bacc
    from concourse.bass_utils import run_bass_kernel_spmd

    L = 60
    arrays, n = layout(np, L, x, src, dst, edge_attr_32, edge_type_8, edge_weight1)
    weights = dict(W0=L0_gnn_W, b0=L0_gnn_b, u=L1_gnn_u, W1=L1_gnn_W1, b1=L1_gnn_b1, W2=L1_gnn_W2, b2=L1_gnn_b2,
                   Wr=L2_gnn_weight_r, attn_l=L3_gnn_attn_l, attn_r=L3_gnn_attn_r)
    arrays.update({k: np.ascontiguousarray(v) for k, v in weights.items()})
    nc = bacc.Bacc("TRN2", target_bir_lowering=False, num_devices=1)
    ins = {k: nc.dram_tensor(f"in_{k}", v.shape, mybir.dt.from_np(v.dtype), kind="ExternalInput").ap() for k, v in arrays.items()}
    out = nc.dram_tensor("out", [n, D], F32, kind="ExternalOutput").ap()
    build(nc, out=out, L=L, **ins)
    r = run_bass_kernel_spmd(nc, [{f"in_{k}": v for k, v in arrays.items()}], core_ids=[0])
    return r.results[0]["out"]


def layout(np, L, x, src, dst, attr, etype, weight):
    n, e = x.shape[0], src.shape[0]
    rows = -(-(n + 1) // (14 * P)) * 14 * P
    J = 6 * L * -(-e // (6 * L * P))
    ep = P * J

    def padded(a, shape, fill, at=0):
        b = np.full(shape, fill, a.dtype)
        b[at:at + a.shape[0]] = a
        return b

    x, src, dst, attr, etype, weight = (np.asarray(a) for a in (x, src, dst, attr, etype, weight))
    keys = padded(dst, (ep + 2,), n, 1)
    keys[0], keys[ep + 1] = -1, -2
    return dict(
        x=padded(x, (rows, x.shape[1]), 0), src=padded(src, (ep,), n).reshape(P, J), dst=keys,
        etype=padded(etype, (ep,), 0).reshape(P, J), weight=padded(weight.reshape(e), (ep,), 0).reshape(P, J),
        attr=padded(attr, (ep, attr.shape[1]), 0)), n
```
